# Optimizing a Trainium2 kernel written in Bass

```python
import numpy as np
import jax
import jax.numpy as jnp

def _softmax(x, axis=-1):
    return jax.nn.softmax(x, axis=axis)

def _gelu(x):
    return jax.nn.gelu(x, approximate=True)

def _silu(x):
    return jax.nn.silu(x)

def _sigmoid(x):
    return jax.nn.sigmoid(x)

def _layernorm(x, axis=-1, eps=1e-05):
    m = jnp.mean(x, axis=axis, keepdims=True)
    v = jnp.var(x, axis=axis, keepdims=True)
    return (x - m) / jnp.sqrt(v + eps)

def _scatter_add(tgt, idx, src, axis=0):
    return tgt.at[idx].add(src)

def _segment_sum(src, seg, n):
    return jax.ops.segment_sum(src, seg, n)
kernel_name = 'mk_flamingo_gated_d1_seqx_r8_fcc532'

def setup_inputs(seed: int=0):
    np.random.seed(seed)
    _w = jnp.asarray

    def _rec_inputs():
        import jax
        import jax.numpy as jnp
        _rk = jax.random.key(seed)
        x = 7.22e-05 + 1 * jax.random.normal(jax.random.fold_in(_rk, 1), (32, 128, 128), jnp.float32)
        _lenS = 128 - jax.random.randint(jax.random.fold_in(_rk, 7), (32,), 0, max(1, 128 // 4) + 1, jnp.int32)
        _lenS2 = 77 - jax.random.randint(jax.random.fold_in(_rk, 8), (32,), 0, max(1, 77 // 4) + 1, jnp.int32)
        _ctx_768P = jax.random.normal(jax.random.fold_in(_rk, 11), (32, 16, 96), jnp.float32)
        _ctx_768c = jax.random.dirichlet(jax.random.fold_in(_rk, 511), 0.3 * jnp.ones((16,), jnp.float32), (32, 77))
        _ctx_768t = jnp.einsum('bsk,bkd->bsd', _ctx_768c, _ctx_768P)
        _ctx_768t = _ctx_768t * jax.lax.rsqrt(jnp.mean(jnp.square(_ctx_768t)) + 1e-12) * 0.953939
        ctx_768 = 3.88148e-05 + 0.999967 * (_ctx_768t + 0.3 * jax.random.normal(jax.random.fold_in(_rk, 611), (32, 77, 96), jnp.float32))
        _validS = jnp.arange(128)[None, :] < _lenS[:, None]
        _validS2 = jnp.arange(77)[None, :] < _lenS2[:, None]
        _causal = jnp.tril(jnp.ones((128, 128), dtype=bool))
        mask_BxS_bf1 = jnp.ones((32, 128), dtype=bool)
        mask_BxS2_bf1 = jnp.ones((32, 77), dtype=bool)
        _g = jax.random.normal(jax.random.fold_in(_rk, 9001), (2, 1), jnp.float32)
        _g = jnp.sign(_g) * jnp.maximum(jnp.abs(_g), 1.0) + (_g == 0) * 1.0
        g_xattn = _g[0]
        g_ffn = _g[1]
        return (x, ctx_768, mask_BxS_bf1, mask_BxS2_bf1, g_xattn, g_ffn)
    x, ctx_768, mask_BxS_bf1, mask_BxS2_bf1, g_xattn, g_ffn = _rec_inputs()

    def _L0_xattn_setup():
        import jax, jax.numpy as jnp
        import numpy as np
        B, T, DT, G, DV = (16, 64, 128, 72, 96)
        H, DH = (4, 32)
        INNER = H * DH
        HID = 4 * DT
        N_STATE = 64
        K_TOP = 32

        def layernorm(x, g, b, eps=1e-05):
            m = x.mean(-1, keepdims=True)
            v = x.var(-1, keepdims=True)
            return (x - m) * jax.lax.rsqrt(v + eps) * g + b

        def s4d(x, log_dt, A_re, A_im, C_re, C_im, D_skip):
            Bb, L, D = x.shape
            dt = jnp.exp(log_dt)
            A = A_re + 1j * A_im
            C = C_re + 1j * C_im
            dtA = dt[:, None] * A
            dC = C * (jnp.exp(dtA) - 1.0) / A
            powers = jnp.exp(dtA[:, :, None] * jnp.arange(L))
            K = 2.0 * jnp.einsum('dn,dnl->dl', dC, powers).real
            n = 2 * L
            Kf = jnp.fft.rfft(K, n=n, axis=-1)
            xf = jnp.fft.rfft(x, n=n, axis=1)
            y = jnp.fft.irfft(xf * Kf.T[None], n=n, axis=1)[:, :L]
            return y + x * D_skip
        key = jax.random.key(seed)
        ks = jax.random.split(key, 16)
        s = 0.02
        inp = {'x_text': jax.random.normal(ks[0], (B, T, DT), jnp.float32), 'x_vision': jax.random.normal(ks[1], (B, G, DV), jnp.float32), 'text_mask': jnp.ones((B, T), bool), 'vision_mask': jnp.ones((B, G), bool), 'Wq': jax.random.normal(ks[2], (DT, INNER), jnp.float32) * s, 'Wk': jax.random.normal(ks[3], (DV, INNER), jnp.float32) * s, 'Wv': jax.random.normal(ks[4], (DV, DT), jnp.float32) * s, 'W_film_in': jax.random.normal(ks[5], (DT, 2 * DT), jnp.float32) * s, 'b_film_in': jnp.zeros((2 * DT,), jnp.float32), 'W_film_out': jax.random.normal(ks[6], (DT, 2 * DT), jnp.float32) * s, 'b_film_out': jnp.zeros((2 * DT,), jnp.float32), 'g_norm_in': jnp.ones((DT,), jnp.float32), 'b_norm_in': jnp.zeros((DT,), jnp.float32), 'g_norm_out': jnp.ones((DT,), jnp.float32), 'b_norm_out': jnp.zeros((DT,), jnp.float32), 'g_ffn': jnp.ones((DT,), jnp.float32), 'b_ffn': jnp.zeros((DT,), jnp.float32), 'W1': jax.random.normal(ks[7], (DT, HID), jnp.float32) * s, 'b1': jnp.zeros((HID,), jnp.float32), 'W2': jax.random.normal(ks[8], (HID, DT), jnp.float32) * s, 'b2': jnp.zeros((DT,), jnp.float32), 'log_dt': jnp.log(0.001) + jax.random.uniform(ks[9], (DT,), jnp.float32) * (jnp.log(0.1) - jnp.log(0.001)), 'A_re': -0.5 * jnp.ones((DT, N_STATE), jnp.float32), 'A_im': jnp.tile(jnp.pi * jnp.arange(N_STATE, dtype=jnp.float32), (DT, 1)), 'C_re': jax.random.normal(ks[10], (DT, N_STATE), jnp.float32) * 0.5 ** 0.5, 'C_im': jax.random.normal(ks[11], (DT, N_STATE), jnp.float32) * 0.5 ** 0.5, 'D_skip': jax.random.normal(ks[12], (DT,), jnp.float32), 'mod_gate': jnp.array(0.5, jnp.float32)}
        return inp
    _L0_xattn_all = _L0_xattn_setup()
    _L0_xattn_in = {k: v for k, v in _L0_xattn_all.items() if k in ('Wq', 'Wk', 'Wv', 'W_film_in', 'b_film_in', 'W_film_out', 'b_film_out', 'g_norm_in', 'b_norm_in', 'g_norm_out', 'b_norm_out', 'g_ffn', 'b_ffn', 'W1', 'b1', 'W2', 'b2', 'log_dt', 'A_re', 'A_im', 'C_re', 'C_im', 'D_skip', 'mod_gate')}
    del _L0_xattn_all

    def _L0_ffn_setup():
        import jax, jax.numpy as jnp
        import numpy as np
        NUM_EXPERTS = 8
        TOP_K = 2
        NUM_GRIDS = 8
        INV_DENOM = 0.5
        GRID = np.linspace(-1.2, 0.2, NUM_GRIDS).astype(np.float32)
        LN_EPS = 1e-05

        def _layernorm(x, g, b):
            mu = x.mean(-1, keepdims=True)
            var = x.var(-1, keepdims=True)
            return (x - mu) * jax.lax.rsqrt(var + LN_EPS) * g + b

        def _rswaf(x, grid):
            t = jnp.tanh((x[..., None] - grid) * INV_DENOM)
            return 1.0 - t * t
        key = jax.random.key(seed)
        ks = jax.random.split(key, 8)
        B, S, H, F = (1, 256, 128, 512)
        F2 = F // 2
        E2 = NUM_EXPERTS // 2
        G = NUM_GRIDS
        s = 0.02
        return {'hidden_states': jax.random.normal(ks[0], (B, S, H), jnp.float32), 'gate_W': jax.random.normal(ks[1], (H, NUM_EXPERTS), jnp.float32) * s, 'mlp_W1': jax.random.normal(ks[2], (E2, H, F), jnp.float32) * s, 'mlp_b1': jnp.zeros((E2, F), jnp.float32), 'mlp_W2': jax.random.normal(ks[3], (E2, F, H), jnp.float32) * s, 'mlp_b2': jnp.zeros((E2, H), jnp.float32), 'kan_ln_g0': jnp.ones((E2, H), jnp.float32), 'kan_ln_b0': jnp.zeros((E2, H), jnp.float32), 'kan_sl_W0': jax.random.normal(ks[4], (E2, H * G, F2), jnp.float32) * s, 'kan_sl_b0': jnp.zeros((E2, F2), jnp.float32), 'kan_ln_g1': jnp.ones((E2, F2), jnp.float32), 'kan_ln_b1': jnp.zeros((E2, F2), jnp.float32), 'kan_sl_W1': jax.random.normal(ks[5], (E2, F2 * G, H), jnp.float32) * s, 'kan_sl_b1': jnp.zeros((E2, H), jnp.float32)}
    _L0_ffn_all = _L0_ffn_setup()
    _L0_ffn_in = {k: v for k, v in _L0_ffn_all.items() if k in ('gate_W', 'mlp_W1', 'mlp_b1', 'mlp_W2', 'mlp_b2', 'kan_ln_g0', 'kan_ln_b0', 'kan_sl_W0', 'kan_sl_b0', 'kan_ln_g1', 'kan_ln_b1', 'kan_sl_W1', 'kan_sl_b1')}
    del _L0_ffn_all
    return {'x': x, 'ctx_768': ctx_768, 'mask_BxS_bf1': mask_BxS_bf1, 'mask_BxS2_bf1': mask_BxS2_bf1, 'g_xattn': g_xattn, 'g_ffn': g_ffn, 'L0_xattn_Wq': _L0_xattn_in['Wq'], 'L0_xattn_Wk': _L0_xattn_in['Wk'], 'L0_xattn_Wv': _L0_xattn_in['Wv'], 'L0_xattn_W_film_in': _L0_xattn_in['W_film_in'], 'L0_xattn_b_film_in': _L0_xattn_in['b_film_in'], 'L0_xattn_W_film_out': _L0_xattn_in['W_film_out'], 'L0_xattn_b_film_out': _L0_xattn_in['b_film_out'], 'L0_xattn_g_norm_in': _L0_xattn_in['g_norm_in'], 'L0_xattn_b_norm_in': _L0_xattn_in['b_norm_in'], 'L0_xattn_g_norm_out': _L0_xattn_in['g_norm_out'], 'L0_xattn_b_norm_out': _L0_xattn_in['b_norm_out'], 'L0_xattn_g_ffn': _L0_xattn_in['g_ffn'], 'L0_xattn_b_ffn': _L0_xattn_in['b_ffn'], 'L0_xattn_W1': _L0_xattn_in['W1'], 'L0_xattn_b1': _L0_xattn_in['b1'], 'L0_xattn_W2': _L0_xattn_in['W2'], 'L0_xattn_b2': _L0_xattn_in['b2'], 'L0_xattn_log_dt': _L0_xattn_in['log_dt'], 'L0_xattn_A_re': _L0_xattn_in['A_re'], 'L0_xattn_A_im': _L0_xattn_in['A_im'], 'L0_xattn_C_re': _L0_xattn_in['C_re'], 'L0_xattn_C_im': _L0_xattn_in['C_im'], 'L0_xattn_D_skip': _L0_xattn_in['D_skip'], 'L0_xattn_mod_gate': _L0_xattn_in['mod_gate'], 'L0_ffn_gate_W': _L0_ffn_in['gate_W'], 'L0_ffn_mlp_W1': _L0_ffn_in['mlp_W1'], 'L0_ffn_mlp_b1': _L0_ffn_in['mlp_b1'], 'L0_ffn_mlp_W2': _L0_ffn_in['mlp_W2'], 'L0_ffn_mlp_b2': _L0_ffn_in['mlp_b2'], 'L0_ffn_kan_ln_g0': _L0_ffn_in['kan_ln_g0'], 'L0_ffn_kan_ln_b0': _L0_ffn_in['kan_ln_b0'], 'L0_ffn_kan_sl_W0': _L0_ffn_in['kan_sl_W0'], 'L0_ffn_kan_sl_b0': _L0_ffn_in['kan_sl_b0'], 'L0_ffn_kan_ln_g1': _L0_ffn_in['kan_ln_g1'], 'L0_ffn_kan_ln_b1': _L0_ffn_in['kan_ln_b1'], 'L0_ffn_kan_sl_W1': _L0_ffn_in['kan_sl_W1'], 'L0_ffn_kan_sl_b1': _L0_ffn_in['kan_sl_b1']}

def reference(x, ctx_768, mask_BxS_bf1, mask_BxS2_bf1, g_xattn, g_ffn, L0_xattn_Wq, L0_xattn_Wk, L0_xattn_Wv, L0_xattn_W_film_in, L0_xattn_b_film_in, L0_xattn_W_film_out, L0_xattn_b_film_out, L0_xattn_g_norm_in, L0_xattn_b_norm_in, L0_xattn_g_norm_out, L0_xattn_b_norm_out, L0_xattn_g_ffn, L0_xattn_b_ffn, L0_xattn_W1, L0_xattn_b1, L0_xattn_W2, L0_xattn_b2, L0_xattn_log_dt, L0_xattn_A_re, L0_xattn_A_im, L0_xattn_C_re, L0_xattn_C_im, L0_xattn_D_skip, L0_xattn_mod_gate, L0_ffn_gate_W, L0_ffn_mlp_W1, L0_ffn_mlp_b1, L0_ffn_mlp_W2, L0_ffn_mlp_b2, L0_ffn_kan_ln_g0, L0_ffn_kan_ln_b0, L0_ffn_kan_sl_W0, L0_ffn_kan_sl_b0, L0_ffn_kan_ln_g1, L0_ffn_kan_ln_b1, L0_ffn_kan_sl_W1, L0_ffn_kan_sl_b1):
    import jax
    import jax.numpy as jnp

    def _L0_xattn_ref(x_text, x_vision, text_mask, vision_mask, Wq, Wk, Wv, W_film_in, b_film_in, W_film_out, b_film_out, g_norm_in, b_norm_in, g_norm_out, b_norm_out, g_ffn, b_ffn, W1, b1, W2, b2, log_dt, A_re, A_im, C_re, C_im, D_skip, mod_gate):
        import jax, jax.numpy as jnp
        import numpy as np
        B, T, DT, G, DV = (16, 64, 128, 72, 96)
        H, DH = (4, 32)
        INNER = H * DH
        HID = 4 * DT
        N_STATE = 64
        K_TOP = 32

        def layernorm(x, g, b, eps=1e-05):
            m = x.mean(-1, keepdims=True)
            v = x.var(-1, keepdims=True)
            return (x - m) * jax.lax.rsqrt(v + eps) * g + b

        def s4d(x, log_dt, A_re, A_im, C_re, C_im, D_skip):
            Bb, L, D = x.shape
            dt = jnp.exp(log_dt)
            A = A_re + 1j * A_im
            C = C_re + 1j * C_im
            dtA = dt[:, None] * A
            dC = C * (jnp.exp(dtA) - 1.0) / A
            powers = jnp.exp(dtA[:, :, None] * jnp.arange(L))
            K = 2.0 * jnp.einsum('dn,dnl->dl', dC, powers).real
            n = 2 * L
            Kf = jnp.fft.rfft(K, n=n, axis=-1)
            xf = jnp.fft.rfft(x, n=n, axis=1)
            y = jnp.fft.irfft(xf * Kf.T[None], n=n, axis=1)[:, :L]
            return y + x * D_skip
        Bb, Tt, D = x_text.shape
        Gg = x_vision.shape[1]
        Q = (x_text @ Wq).reshape(Bb, Tt, H, DH)
        K = (x_vision @ Wk).reshape(Bb, Gg, H, DH)
        scores = jnp.einsum('bthd,bghd->bhtg', Q, K) / np.sqrt(DH).astype(np.float32)
        scores = jnp.where(vision_mask[:, None, None, :], scores, -jnp.inf)
        topv, topi = jax.lax.top_k(scores, K_TOP)
        probs = jax.nn.softmax(topv, axis=-1)
        bi = jnp.arange(Bb)[:, None, None, None]
        hi = jnp.arange(H)[None, :, None, None]
        ti = jnp.arange(Tt)[None, None, :, None]
        attn = jnp.zeros_like(scores).at[bi, hi, ti, topi].set(probs)
        attn_mean = attn.mean(axis=1)
        V = x_vision @ Wv
        c_t = jnp.einsum('btg,bgd->btd', attn_mean, V)
        c_t = c_t * text_mask[..., None]
        x = layernorm(x_text, g_norm_in, b_norm_in)
        scale_in, shift_in = jnp.split(c_t @ W_film_in + b_film_in, 2, axis=-1)
        x = x * (1.0 + mod_gate * scale_in) + mod_gate * shift_in
        y = s4d(x, log_dt, A_re, A_im, C_re, C_im, D_skip)
        scale_out, shift_out = jnp.split(c_t @ W_film_out + b_film_out, 2, axis=-1)
        y = y * (1.0 + mod_gate * scale_out) + mod_gate * shift_out
        xt = x_text + y
        h = layernorm(xt, g_ffn, b_ffn)
        h = jax.nn.gelu(h @ W1 + b1, approximate=False) @ W2 + b2
        xt = xt + h
        return layernorm(xt, g_norm_out, b_norm_out)

    def _L0_ffn_ref(hidden_states, gate_W, mlp_W1, mlp_b1, mlp_W2, mlp_b2, kan_ln_g0, kan_ln_b0, kan_sl_W0, kan_sl_b0, kan_ln_g1, kan_ln_b1, kan_sl_W1, kan_sl_b1):
        import jax, jax.numpy as jnp
        import numpy as np
        NUM_EXPERTS = 8
        TOP_K = 2
        NUM_GRIDS = 8
        INV_DENOM = 0.5
        GRID = np.linspace(-1.2, 0.2, NUM_GRIDS).astype(np.float32)
        LN_EPS = 1e-05

        def _layernorm(x, g, b):
            mu = x.mean(-1, keepdims=True)
            var = x.var(-1, keepdims=True)
            return (x - mu) * jax.lax.rsqrt(var + LN_EPS) * g + b

        def _rswaf(x, grid):
            t = jnp.tanh((x[..., None] - grid) * INV_DENOM)
            return 1.0 - t * t
        B, S, H = hidden_states.shape
        E2, _, F2 = (kan_sl_W0.shape[0], kan_sl_W0.shape[1], kan_sl_W0.shape[2])
        G = NUM_GRIDS
        x = hidden_states.reshape(-1, H)
        T = x.shape[0]
        logits = x @ gate_W
        probs = jax.nn.softmax(logits.astype(jnp.float32), axis=-1)
        rw, sel = jax.lax.top_k(probs, TOP_K)
        rw = rw / rw.sum(axis=-1, keepdims=True)
        w_full = jnp.sum(jax.nn.one_hot(sel, NUM_EXPERTS, dtype=rw.dtype) * rw[..., None], axis=1)
        w_full = w_full.astype(x.dtype)
        h = jnp.einsum('th,ehf->etf', x, mlp_W1) + mlp_b1[:, None, :]
        h = jax.nn.gelu(h, approximate=False)
        mlp_out = jnp.einsum('etf,efh->eth', h, mlp_W2) + mlp_b2[:, None, :]
        grid = jnp.asarray(GRID)
        h0 = _layernorm(x[None], kan_ln_g0[:, None, :], kan_ln_b0[:, None, :])
        basis0 = _rswaf(h0, grid).reshape(E2, T, H * G)
        z = jnp.einsum('eti,eio->eto', basis0, kan_sl_W0) + kan_sl_b0[:, None, :]
        h1 = _layernorm(z, kan_ln_g1[:, None, :], kan_ln_b1[:, None, :])
        basis1 = _rswaf(h1, grid).reshape(E2, T, F2 * G)
        kan_out = jnp.einsum('eti,eio->eto', basis1, kan_sl_W1) + kan_sl_b1[:, None, :]
        expert_out = jnp.concatenate([mlp_out, kan_out], axis=0)
        out = jnp.einsum('eth,te->th', expert_out, w_full)
        return out.reshape(B, S, H)
    x = x + jnp.tanh(g_xattn[0]) * _L0_xattn_ref(_layernorm(x, axis=-1), ctx_768, mask_BxS_bf1, mask_BxS2_bf1, L0_xattn_Wq, L0_xattn_Wk, L0_xattn_Wv, L0_xattn_W_film_in, L0_xattn_b_film_in, L0_xattn_W_film_out, L0_xattn_b_film_out, L0_xattn_g_norm_in, L0_xattn_b_norm_in, L0_xattn_g_norm_out, L0_xattn_b_norm_out, L0_xattn_g_ffn, L0_xattn_b_ffn, L0_xattn_W1, L0_xattn_b1, L0_xattn_W2, L0_xattn_b2, L0_xattn_log_dt, L0_xattn_A_re, L0_xattn_A_im, L0_xattn_C_re, L0_xattn_C_im, L0_xattn_D_skip, L0_xattn_mod_gate)
    x = x + jnp.tanh(g_ffn[0]) * _L0_ffn_ref(_layernorm(x, axis=-1), L0_ffn_gate_W, L0_ffn_mlp_W1, L0_ffn_mlp_b1, L0_ffn_mlp_W2, L0_ffn_mlp_b2, L0_ffn_kan_ln_g0, L0_ffn_kan_ln_b0, L0_ffn_kan_sl_W0, L0_ffn_kan_sl_b0, L0_ffn_kan_ln_g1, L0_ffn_kan_ln_b1, L0_ffn_kan_sl_W1, L0_ffn_kan_sl_b1)
    return x

_drawn_inputs = setup_inputs


def setup_inputs(seed=0):
    import zlib

    import numpy as np

    out = dict(_drawn_inputs(seed))
    spreads = {'L0_xattn_b_film_in': (0.0, 0.1),
     'L0_xattn_b_film_out': (0.0, 0.1),
     'L0_xattn_g_norm_in': (1.0, 0.2),
     'L0_xattn_b_norm_in': (0.0, 0.1),
     'L0_xattn_g_norm_out': (1.0, 0.2),
     'L0_xattn_b_norm_out': (0.0, 0.1),
     'L0_xattn_g_ffn': (1.0, 0.6),
     'L0_xattn_b_ffn': (0.0, 0.8),
     'L0_xattn_b1': (0.0, 0.413),
     'L0_xattn_b2': (0.0, 0.1),
     'L0_xattn_A_re': (-0.5, 0.2),
     'L0_ffn_mlp_b1': (0.0, 0.8),
     'L0_ffn_mlp_b2': (0.0, 0.1),
     'L0_ffn_kan_ln_g0': (1.0, 0.6),
     'L0_ffn_kan_ln_b0': (0.0, 2.0),
     'L0_ffn_kan_sl_b0': (0.0, 0.54),
     'L0_ffn_kan_ln_g1': (1.0, 0.6),
     'L0_ffn_kan_ln_b1': (0.0, 0.8),
     'L0_ffn_kan_sl_b1': (0.0, 0.301)}
    factors = {'ctx_768': 3.221,
     'L0_xattn_Wq': 7.89,
     'L0_xattn_Wk': 8.0,
     'L0_xattn_Wv': 3.38,
     'L0_xattn_W_film_in': 3.704,
     'L0_xattn_W_film_out': 4.764,
     'L0_ffn_mlp_W1': 3.677,
     'L0_ffn_mlp_W2': 3.306}
    for name, (base, spread) in spreads.items():
        noise = np.random.default_rng([zlib.crc32(name.encode()), seed]).standard_normal(out[name].shape)
        drawn = base * np.exp(spread * noise) if base else spread * noise
        out[name] = jnp.asarray(drawn.astype(out[name].dtype))
    for name, factor in factors.items():
        out[name] = (out[name] * factor).astype(out[name].dtype)
    return out
```

```python
from contextlib import ExitStack

import numpy as np

import concourse.bass as bass
from concourse import mybir

F32 = mybir.dt.float32
BF16 = mybir.dt.bfloat16
U8 = mybir.dt.uint8
U32 = mybir.dt.uint32
I32 = mybir.dt.int32
ALU = mybir.AluOpType
ACT = mybir.ActivationFunctionType
AX = mybir.AxisListType

P = 128
S = 128
D = 128
G = 4
GT = G * S
NK = 77
DV = 96
H = 4
DH = 32
TOPK = 32
HID = 512
HC = HID // P
NE = 4
NX = 2 * NE
NG = 8
F2 = 256
NST = 64
NB = 16
NA = S // NB
EPS = 1e-5
SCALE = float(1.0 / np.sqrt(np.float32(DH)))
BIG = 1e30
GUARD = -1e29
TAKEN = -3.0e38
ROUND = 12582912.0
TWO_PI = 6.2831845
LOG2E, LN2_HI, LN2_LO = 1.4426950408889634, 0.693359375, -2.12194440e-4
RING = 8
STEP = 4

VECS = [("L0_ffn_kan_ln_g0", NE), ("L0_ffn_kan_ln_b0", NE), ("L0_ffn_kan_ln_g1", 2 * NE), ("L0_ffn_kan_ln_b1", 2 * NE),
        ("L0_ffn_kan_sl_b0", 2 * NE), ("L0_ffn_kan_sl_b1", NE), ("L0_ffn_mlp_b1", HC * NE), ("L0_ffn_mlp_b2", NE),
        ("L0_xattn_b1", HC), ("L0_xattn_g_ffn", 1), ("L0_xattn_b_ffn", 1)]
ROW_OF, _r = {}, 0
for _n, _k in VECS:
    ROW_OF[_n] = _r
    _r += _k
NROWS = _r

CHUNKS = [(e, layer, k) for e, layer in [(0, 0), (1, 0), (0, 1), (2, 0), (1, 1), (3, 0), (2, 1), (3, 1)]
          for k in range(NG * (layer + 1))]
OUTS = [0, 1, NE, 2, NE + 1, 3, NE + 2, NE + 3]


def mixture_steps():
    u = ("use",)
    it = [("start",), ("make",), ("gate_a",), ("gate_b",), ("make",), ("gate_c",),
          u, ("gate_d",), u, ("z_out", 0), ("wb", 0), ("mlp", 0), ("wb", 1), ("comb", 0),
          ("var_a", 0), u, ("var_b", 0), ("wb", 2), u, ("z_out", 1), ("mlp", 1), ("comb", 1)]
    for e in (1, 2, 3):
        it += [("var_a", e), u, u, ("var_b", e), u, u, ("comb", 2 * e)]
        if e < 3:
            it += [("wb", 2 * e + 1), u, ("wb", 2 * e + 2), u, ("z_out", e + 1), ("mlp", e + 1), ("comb", 2 * e + 1)]
        else:
            it += [("wb", 7), u, u, u, u, ("comb", 7), ("finish",)]
    made, used, res = 2 * STEP, 0, []
    for s in it:
        res.append(s)
        used += STEP * (s == u)
        while made < min(used + RING, len(CHUNKS)):
            e, layer, _ = CHUNKS[made]
            if layer == 1 and ("var_b", e) not in res:
                break
            res.append(("make",))
            made += STEP
    assert made == len(CHUNKS) and STEP * it.count(u) == len(CHUNKS)
    return res


def attention_steps():
    res = [("load",), ("ln1",), ("ln1_out",), ("qk_turn",), ("qk",), ("vwf",), ("scores", 0), ("scores", 2)]
    res += [("topk", b, r) for b in range(G) for r in range(TOPK // 8)]
    res += [("probs_a",), ("probs_b",), ("probs_c",), ("attn_turn",), ("film",), ("modulate",), ("conv_a",), ("conv_b",),
            ("conv_c",), ("conv_d",), ("ln2",), ("ln2_out",), ("ht_turn",), ("xmlp_a",), ("xmlp_b",), ("ln3",), ("ln3_out",),
            ("ln4",), ("ln4_out",), ("xt_turn",)]
    return res


def both_steps():
    moe, att = mixture_steps(), attention_steps()
    late = att.index(("ln4",))
    slots = sum(s[0] in ("use", "mlp") for s in moe)
    res, k, seen = [], 1, 0
    for s in moe:
        res.append(s)
        if s[0] == "start":
            res.append(att[0])
        if s[0] in ("use", "mlp"):
            seen += 1
            want = 1 + round((late - 1) * min(1.0, seen / (slots - 1)))
            res += att[k:want]
            k = max(k, want)
    return res + att[k:]


def build(nc, a, out):
    NROW = a["x"].shape[0]
    NGROUPS = NROW // G
    kscratch = nc.dram_tensor("k_scratch", (S, D), F32, kind="Internal").ap()

    with ExitStack() as ctx:
        def sb(name, shape, dt=F32):
            return ctx.enter_context(nc.sbuf_tensor(name, shape, dt))

        def bank(name):
            return ctx.enter_context(nc.psum_tensor(name, [P, GT], F32))

        def sem(name):
            return ctx.enter_context(nc.semaphore(name))

        kw0 = sb("kw0", [P, NE, NG, F2])
        kw1 = sb("kw1", [P, NE, 2 * NG, D])
        mw1 = sb("mw1", [P, NE, HID])
        mw2 = sb("mw2", [P, NE, HC, D])
        gatew = sb("gatew", [P, NX])
        wq = sb("wq", [P, P])
        wk = sb("wk", [P, P])
        wvf = sb("wvf", [P, 4 * D])
        xw1 = sb("xw1", [P, HID])
        xw2 = sb("xw2", [P, HC, D])
        dft = sb("dft", [P, 4, P])
        kf = sb("kf", [P, 2, D])
        ident = sb("ident", [P, P])
        identb = sb("identb", [P, P], BF16)
        ones = sb("ones", [P, P])
        mean_w = sb("mean_w", [P, P])
        esel = sb("esel", [3 * NX, NX, P], BF16)
        misc = sb("misc", [P, 17])
        cols = sb("cols", [P, NROWS])
        scale0 = sb("scale0", [P, NE])
        bias0 = sb("bias0", [P, NE, NG])
        scale1 = sb("scale1", [P, 2 * NE])
        bias1 = sb("bias1", [P, 2 * NE, NG])
        const0 = sb("const0", [P, NE, 2])
        const1 = sb("const1", [P, NE])
        xb1 = sb("xb1", [P, HC])
        gout = sb("gout", [P, D])
        bout = sb("bout", [P, D])
        b2row = sb("b2row", [P, D])
        tmt = sb("tmt", [P, NROW])
        gates = sb("gates", [P, 3])
        gtanh = sb("gtanh", [P, 2])
        minus_half = sb("minus_half", [P, G])
        xg = sb("xg", [P, G, D])
        cg = sb("cg", [NK, G, DV])
        vmu = sb("vmu", [P, G * NK], U8)
        vmb = sb("vmb", [P, G * NK])
        tmg = sb("tmg", [P, G])
        x0 = sb("x0", [P, G, D])
        xh = sb("xh", [P, G, D])
        x0t = sb("x0t", [P, GT])
        ct = sb("ct", [P, G, NK + 1])
        qt = sb("qt", [P, GT])
        kblk = sb("kblk", [P, G, H, NK])
        vwf = sb("vwf", [P, G, 4 * D])
        scr = sb("scr", [P, G, H, NK])
        left = sb("left", [P, G, H, NK])
        top = sb("top", [P, G, H, 2, 8])
        attn = sb("attn", [P, G, NK + 1])
        attnt = sb("attnt", [P, GT])
        film = sb("film", [P, G, 4 * D])
        xnew = sb("xnew", [P, G, D])
        st = sb("st", [P, G, 6])
        mv = sb("mv", [P, G, 2])
        sml = sb("sml", [P, 16, G])
        sm16 = sb("sm16", [P, 4, G * H])
        xft = sb("xft", [P, GT])
        xkt = sb("xkt", [P, GT])
        xres = sb("xres", [P, G, D])
        ring = sb("ring", [P, RING, GT])
        zc = sb("zc", [P, 2, GT])
        zq = sb("zq", [P, 2, GT])
        h1 = sb("h1", [P, 2, 2, GT])
        dg = sb("dg", [P, G, P])
        vv = sb("vv", [P, 2, G])
        mg = sb("mg", [P, 2, GT])
        wbs = sb("wbs", [P, 3, GT])
        part = sb("part", [P, 2, GT])
        acc = sb("acc", [P, GT])
        gl = sb("gl", [P, G, NX])
        gtop = sb("gtop", [P, G, 8])
        gidx = sb("gidx", [P, G, 8], U32)
        gidf = sb("gidf", [P, G, 8])
        gs = sb("gs", [P, 5, G])
        gw = sb("gw", [P, 5, G, NX])
        wp = sb("wp", [P, G, 3, NX], BF16)
        wt = sb("wt", [3 * NX, GT], BF16)
        xm = qt[:, :].rearrange("p (b d) -> p b d", b=G)
        hh = x0t[:, :].rearrange("p (b d) -> p b d", b=G)
        ht = attnt
        spec = vwf
        gx = vwf
        xt = x0
        yout = wbs[:, 0, :].rearrange("p (b d) -> p b d", b=G)
        pw_r = ring[:, 0:4, :].rearrange("p a b -> p (a b)").rearrange("p (n d) -> p n d", n=NB)
        pw_e = ring[:, 4:8, :].rearrange("p a b -> p (a b)").rearrange("p (n d) -> p n d", n=NB)
        pw_cs = film[:, :, :].rearrange("p a b -> p (a b)").rearrange("p (c n d) -> p c n d", c=2, n=NA)
        rounded = h1[:, :, :, :].rearrange("p a b c -> p (a b c)")
        pw_a = zc[:, :, :].rearrange("p a b -> p (a b)").rearrange("p (n d) -> p n d", n=NA)
        pw_t = zq[:, :, :].rearrange("p a b -> p (a b)").rearrange("p (n d) -> p n d", n=NA)
        ka = h1[0:NA, :, :, :].rearrange("p a b c -> p (a b c)").rearrange("p (n d) -> p n d", n=NB)
        kl = mg[:, 0, 0:D]
        vflat = vwf[:, :, :].rearrange("p a b -> p (a b)")
        stack_d = vflat[:, 0:512].rearrange("p (k c) -> p k c", k=4)
        s4in = vflat[:, 512:768].rearrange("p (k n) -> p k n", k=4)
        s4t = vflat[:, 768:2048].rearrange("p (k n) -> p k n", n=NST)
        stk = acc[:, :].rearrange("p (k d) -> p k d", k=4)
        wfs = part[:, 0, :]
        wvin = part[:, 1, 0:D]
        wvt = part[:, 1, D:2 * D]
        wfilm = dg[:, :, :].rearrange("p a b -> p (a b)")
        gnin = xh[:, 0, :]
        bnin = xh[:, 1, :]
        vrows = xh[:, 2, :]
        tm_u8 = vmu[0:NROW, 0:S]
        tm_rows = xh[0:NROW, 3, :]
        sflat = scr[:, :, :, :].rearrange("p a b c -> p (a b c)")
        brow = sflat[0:1, 0:512]
        brow2 = sflat[0:1, 512:1024]
        lflat = left[:, :, :, :].rearrange("p a b c -> p (a b c)")
        drow = lflat[0:1, 0:D]
        onehot = lflat[0:1, D:D + DV + 1]
        esel_in = mg[0:3 * NX, :, :].rearrange("p a b -> p (a b)").rearrange("p (k m) -> p k m", k=NX)
        tiny = sml[:, :, :].rearrange("p a b -> p (a b)")
        tiny_i = sb("tiny_i", [P, 1], I32)
        rsum = sb("rsum", [P, NE, NG])

        Z = [bank("Z0"), bank("Z1")]
        HA, V, O, XA, XB, XC = bank("HA"), bank("V"), bank("O"), bank("XA"), bank("XB"), bank("XC")

        in_const, in_s4, in_attn, in_film, in_xmlp, in_vec, in_moe, in_kw1 = [
            sem("in_" + n) for n in ("const", "s4", "attn", "film", "xmlp", "vec", "moe", "kw1")]
        in_kw0 = [sem(f"in_kw0_{e}") for e in range(NE)]
        set_dve, set_pool = sem("set_dve"), sem("set_pool")
        tanh_r, tanh_ar, sin_half, stack_made, stack_ps, stack_sb = [
            sem(n) for n in ("tanh_r", "tanh_ar", "sin_half", "stack_made", "stack_ps", "stack_sb")]
        r_ready, dt_args, half_args = sem("r_ready"), sem("dt_args"), sem("half_args")
        fine_args, fine_sin, fine_exp, fine_pow = sem("fine_args"), sem("fine_sin"), sem("fine_exp"), sem("fine_pow")
        coarse_args, coarse_sin, coarse_exp, coarse_pow = sem("coarse_args"), sem("coarse_sin"), sem("coarse_exp"), sem("coarse_pow")
        k_taps_ps, k_taps_sb, k_out, k_back, kf_ps = sem("k_taps_ps"), sem("k_taps_sb"), sem("k_out"), sem("k_back"), sem("kf_ps")
        ones_made, vec_ps, vec_sb, wv_ps, wv_sb = sem("ones_made"), sem("vec_ps"), sem("vec_sb"), sem("wv_ps"), sem("wv_sb")
        film_w, wvf_ps, tm_made, tm_ps, b1_ps = sem("film_w"), sem("wvf_ps"), sem("tm_made"), sem("tm_ps"), sem("b1_ps")
        row_sums, centred, const_ps, gates_tanh = sem("row_sums"), sem("centred"), sem("const_ps"), sem("gates_tanh")

        x_in = sem("x_in")
        ctx_in, vmask_in, out_sent = sem("ctx_in"), sem("vmask_in"), sem("out_sent")
        dve_own, pool_own = sem("dve_own"), sem("pool_own")
        ln_stats, ln_scales, x0_ready, x0t_ps, ct_ps, x0t_sb, ct_sb, q_ps, q_sb, k_ps, k_sb = [sem(n) for n in (
            "ln_stats", "ln_scales", "x0_ready", "x0t_ps", "ct_ps", "x0t_sb", "ct_sb", "q_ps", "q_sb", "k_ps", "k_sb")]
        vwf_ps, vwf_sb, sc_ps, sc_sb, guard_ready, diff_ready, exp_ready, recip_ready, prob_ready, attn_ready = [sem(n) for n in (
            "vwf_ps", "vwf_sb", "sc_ps", "sc_sb", "guard_ready", "diff_ready", "exp_ready", "recip_ready", "prob_ready", "attn_ready")]
        at_ps, at_sb, film_ps, film_sb, xm_ready, xd_ready, spec_ps, spec_mul, spec_ready = [sem(n) for n in (
            "at_ps", "at_sb", "film_ps", "film_sb", "xm_ready", "xd_ready", "spec_ps", "spec_mul", "spec_ready")]
        y_ps, y_mod, xt_ready, hh_ready, ht_ps, ht_sb, xh_ps, gx_done, xo_ps, xo_add, xt2_ready = [sem(n) for n in (
            "y_ps", "y_mod", "xt_ready", "hh_ready", "ht_ps", "ht_sb", "xh_ps", "gx_done", "xo_ps", "xo_add", "xt2_ready")]
        n_ready, xnew_ready, xf_ready, xft_ps, xt_turned = [sem(n) for n in (
            "n_ready", "xnew_ready", "xf_ready", "xft_ps", "xt_turned")]
        res_ready, gl_ps, gl_sb, gdiff, gexp, wp_ready, wt_ps, wt_sb, wb_ps, wb_sb = [sem(n) for n in (
            "res_ready", "gl_ps", "gl_sb", "gdiff", "gexp", "wp_ready", "wt_ps", "wt_sb", "wb_ps", "wb_sb")]
        tanh_done, basis_ready, basis_used, l0_ps, zc_ready, zq_ready, var_ps, var_sb, rstd_ready, dg_ready, rb_ps, h1_ready = [
            sem(n) for n in ("tanh_done", "basis_ready", "basis_used", "l0_ps", "zc_ready", "zq_ready", "var_ps", "var_sb",
                             "rstd_ready", "dg_ready", "rb_ps", "h1_ready")]
        mh_ps, mg_done, mg_used, o_ps, part_ready, acc_ready, yt_ps, y_ready = [sem(n) for n in (
            "mh_ps", "mg_done", "mg_used", "o_ps", "part_ready", "acc_ready", "yt_ps", "y_ready")]
        arrive = sem("arrive")
        round_sems = range(x_in.num, arrive.num + 1)
        go = {n: sem("go_" + n) for n in ("tensor", "scalar", "vector", "gpsimd")}

        block = ctx.enter_context(nc.Block())

        STEPS = {"attention": attention_steps(), "mixture": mixture_steps(), "both": both_steps()}

        def meet(eng, name):
            if name == "sync":
                eng.wait_ge(arrive, 4)
                eng.sem_clear(round_sems)
                for s in go.values():
                    eng.sem_inc(s, 1)
            else:
                eng.drain().then_inc(arrive, 1)
                eng.wait_ge(go[name], 1)
                eng.sem_clear(go[name])

        def rounds(eng, name, steps, counts):
            def one(kind, mixed, attended):
                counts.clear()
                counts.update(made=0, used=0, hidden=0, wb=0, out=0, own=0, h1=0)
                for s in STEPS[kind]:
                    if s[0] in steps:
                        steps[s[0]](mixed, attended, *s[1:])
                if kind != "attention" and "end" in steps:
                    steps["end"](mixed, attended)
                meet(eng, name)

            meet(eng, name)
            one("attention", None, 0)
            with eng.Fori(0, NGROUPS - 1) as i:
                one("both", i, i + 1)
            one("mixture", NGROUPS - 1, None)

        @block.sync
        def _(sp):
            for dst, src in ((misc[:, :], a["c_misc"]), (ident[:, :], a["c_ident"]), (dft[:, :, :], a["c_dft"]),
                             (esel_in, a["c_esel"])):
                sp.dma_start(dst, src).then_inc(in_const, 16)
            sp.dma_start(tiny[:, 0:1], a["L0_xattn_log_dt"].rearrange("(p a) -> p a", a=1)).then_inc(in_s4, 16)
            for k, n in enumerate(("A_re", "A_im", "C_re", "C_im")):
                sp.dma_start(s4in[:, k, :], a["L0_xattn_" + n]).then_inc(in_s4, 16)
            sp.dma_start(drow, a["L0_xattn_D_skip"].rearrange("(a p) -> a p", a=1)).then_inc(in_s4, 16)
            sp.dma_start(wvin[0:DV, :], a["L0_xattn_Wv"]).then_inc(in_film, 16)
            sp.dma_start(wfilm[:, 0:2 * D], a["L0_xattn_W_film_in"]).then_inc(in_film, 16)
            sp.dma_start(wfilm[:, 2 * D:4 * D], a["L0_xattn_W_film_out"]).then_inc(in_film, 16)
            sp.dma_start(brow[:, 0:2 * D], a["L0_xattn_b_film_in"].rearrange("(a n) -> a n", a=1)).then_inc(in_film, 16)
            sp.dma_start(brow[:, 2 * D:4 * D], a["L0_xattn_b_film_out"].rearrange("(a n) -> a n", a=1)).then_inc(in_film, 16)
            sp.dma_start(gnin, a["L0_xattn_g_norm_in"].partition_broadcast(P)).then_inc(in_film, 16)
            sp.dma_start(bnin, a["L0_xattn_b_norm_in"].partition_broadcast(P)).then_inc(in_film, 16)
            sp.dma_start(gates[:, 0:1], a["L0_xattn_mod_gate"].partition_broadcast(P)).then_inc(in_film, 16)
            sp.dma_start(gates[:, 1:2], a["g_xattn"].partition_broadcast(P)).then_inc(in_film, 16)
            sp.dma_start(gates[:, 2:3], a["g_ffn"].partition_broadcast(P)).then_inc(in_film, 16)
            for n, k in VECS:
                src = a[n].rearrange("e (h p) -> (e h) p", p=P) if len(a[n].shape) == 2 else a[n].rearrange("(h p) -> h p", p=P)
                sp.dma_start(vrows[ROW_OF[n]:ROW_OF[n] + k, :], src).then_inc(in_vec, 16)
            sp.dma_start(xw1[:, :], a["L0_xattn_W1"]).then_inc(in_xmlp, 16)
            sp.dma_start(xw2[:, :, :], a["L0_xattn_W2"].rearrange("(c p) d -> p c d", p=P)).then_inc(in_xmlp, 16)
            sp.dma_start(gout[:, :], a["L0_xattn_g_norm_out"].partition_broadcast(P)).then_inc(in_xmlp, 16)
            sp.dma_start(bout[:, :], a["L0_xattn_b_norm_out"].partition_broadcast(P)).then_inc(in_xmlp, 16)
            sp.dma_start(b2row[:, :], a["L0_xattn_b2"].partition_broadcast(P)).then_inc(in_xmlp, 16)
            sp.dma_start(wq[:, :], a["L0_xattn_Wq"]).then_inc(in_attn, 16)
            sp.dma_start(wk[0:DV, :], a["L0_xattn_Wk"]).then_inc(in_attn, 16)
            sp.dma_start(tm_u8, a["mask_text"]).then_inc(in_attn, 16)
            for e in range(NE):
                sp.dma_start(kw0[:, e, :, :], a["L0_ffn_kan_sl_W0"][e].rearrange("(p g) o -> p g o", g=NG)).then_inc(in_kw0[e], 16)
            for e in range(NE):
                for h in range(2):
                    sp.dma_start(kw1[:, e, h * NG:(h + 1) * NG, :],
                                 a["L0_ffn_kan_sl_W1"][e].rearrange("(h p g) o -> h p g o", h=2, g=NG)[h]).then_inc(in_kw1, 16)
            sp.dma_start(gatew[:, :], a["L0_ffn_gate_W"]).then_inc(in_moe, 16)
            for e in range(NE):
                sp.dma_start(mw1[:, e, :], a["L0_ffn_mlp_W1"][e]).then_inc(in_moe, 16)
                sp.dma_start(mw2[:, e, :, :], a["L0_ffn_mlp_W2"][e].rearrange("(c p) o -> p c o", p=P)).then_inc(in_moe, 16)
            sp.wait_ge(k_taps_sb, 4)
            sp.dma_start(kscratch.rearrange("(a b) d -> a b d", a=NA), ka).then_inc(k_out, 16)
            sp.wait_ge(k_out, 16)
            sp.wait_ge(set_dve, 1)
            sp.dma_start(kl, kscratch).then_inc(k_back, 16)
            sp.wait_ge(in_moe, 16 * (1 + 2 * NE))

            def load(mixed, g):
                sp.dma_start(xg[:, :, :], a["x"].rearrange("(n b) s d -> n s b d", b=G)[g]).then_inc(x_in, 16)
                sp.dma_start(cg[:, :, :], a["ctx_768"].rearrange("(n b) s d -> n s b d", b=G)[g]).then_inc(ctx_in, 16)
                sp.dma_start(vmu[:, :], a["mask_vision"].rearrange("(n b) k -> n (b k)", b=G)[g].partition_broadcast(P))\
                  .then_inc(vmask_in, 16)

            def finish(g, attended):
                sp.wait_ge(y_ready, 1)
                sp.dma_start(out.rearrange("(n b) s d -> n s b d", b=G)[g], yout).then_inc(out_sent, 16)

            def end(g, attended):
                sp.wait_ge(out_sent, 16)

            rounds(sp, "sync", {"load": load, "finish": finish, "end": end}, {})

        @block.tensor
        def _(pe):
            n = {}

            pe.wait_ge(in_const, 64)
            pe.wait_ge(in_vec, 16 * len(VECS))
            pe.transpose(XA[:, 0:NROWS], vrows[0:NROWS, :], ident[0:NROWS, 0:NROWS]).then_inc(vec_ps, 1)
            pe.wait_ge(in_film, 160)
            pe.transpose(XB[:, 0:DV], wvin[0:DV, :], ident[0:DV, 0:DV]).then_inc(wv_ps, 1)
            pe.wait_ge(tm_made, 1)
            pe.transpose(HA[:, 0:NROW], tm_rows, ident[0:NROW, 0:NROW]).then_inc(tm_ps, 1)
            pe.wait_ge(stack_made, 4)
            for k in range(4):
                t = pe.transpose(XC[:, k * P:(k + 1) * P], stack_d[:, k, :], ident[:, :])
            t.then_inc(stack_ps, 1)
            pe.wait_ge(in_xmlp, 80)
            pe.wait_ge(vec_sb, 1)
            bf = cols[:, ROW_OF["L0_xattn_b_ffn"]:ROW_OF["L0_xattn_b_ffn"] + 1]
            for c in range(HC):
                t = pe.matmul(V[:, c:c + 1], xw1[:, c * P:(c + 1) * P], bf, start=True, stop=True)
            t.then_inc(b1_ps, 1)
            pe.wait_ge(film_w, 3)
            pe.wait_ge(wv_sb, 1)
            pe.matmul(O[0:DV + 1, :], wvt[:, 0:DV + 1], wfs, start=True, stop=False)
            pe.matmul(O[0:DV + 1, :], onehot, brow2, start=False, stop=True).then_inc(wvf_ps, 1)
            pe.wait_ge(fine_pow, 1)
            pe.wait_ge(coarse_pow, 1)
            pe.wait_ge(set_dve, 2)
            pe.wait_ge(wv_sb, 2)
            for q, bk in enumerate((Z[0], Z[1], HA, V)):
                for d in range(32):
                    t = pe.matmul(bk[0:NA, d * NB:(d + 1) * NB], pw_a[:, :, 32 * q + d], pw_r[:, :, 32 * q + d],
                                  start=True, stop=True)
                t.then_inc(k_taps_ps, 1)
            pe.wait_ge(k_back, 16)
            pe.wait_ge(ones_made, 3)
            pe.matmul(XB[:, 0:D], dft[:, 0, :], kl, start=True, stop=False)
            pe.matmul(XB[:, 0:D], ones[0:1, :], drow, start=False, stop=True)
            pe.matmul(XB[:, D:2 * D], dft[:, 1, :], kl, start=True, stop=True).then_inc(kf_ps, 1)
            for e in range(NE):
                pe.wait_ge(centred, e + 1)
                for h in range(2):
                    for g in range(NG):
                        pe.matmul(XA[:, 2 * e + h:2 * e + h + 1], kw0[:, e, g, h * P:(h + 1) * P], ones[:, 0:1],
                                  start=(g == 0), stop=(g == NG - 1))
            pe.wait_ge(in_kw1, 32 * NE)
            for e in range(NE):
                for k in range(2 * NG):
                    pe.matmul(XA[:, 2 * NE + e:2 * NE + e + 1], kw1[:, e, k, :], ones[:, 0:1],
                              start=(k == 0), stop=(k == 2 * NG - 1))
            sb0 = cols[:, ROW_OF["L0_ffn_kan_sl_b0"]:ROW_OF["L0_ffn_kan_sl_b0"] + 2 * NE].rearrange("p (e h) -> p h e", h=2)
            for h in range(2):
                t = pe.matmul(XA[:, 3 * NE:4 * NE], mean_w[:, :], sb0[:, h, :], start=(h == 0), stop=(h == 1))
            t.then_inc(const_ps, 1)

            def qk_turn(m, g):
                pe.wait_ge(x0_ready, 1)
                for b in range(G):
                    t = pe.transpose(XA[:, b * S:(b + 1) * S], x0[:, b, :], ident[:, :])
                t.then_inc(x0t_ps, 1)
                pe.wait_ge(ctx_in, 16)
                for b in range(G):
                    t = pe.transpose(XB[0:DV, b * NK:(b + 1) * NK], cg[:, b, :], ident[0:NK, 0:NK])
                t.then_inc(ct_ps, 1)

            def qk(m, g):
                pe.wait_ge(x0t_sb, 1)
                pe.matmul(XA[:, :], wq[:, :], x0t[:, :], start=True, stop=True).then_inc(q_ps, 1)
                pe.wait_ge(ct_sb, 1)
                pe.matmul(XB[:, 0:G * NK].rearrange("p (b k) -> p b k", b=G), wk[0:DV, :], ct[0:DV, :, 0:NK],
                          start=True, stop=True).then_inc(k_ps, 1)

            def vwf_(m, g):
                for b, bk in enumerate((XC, XA, XB, XC)):
                    if b == 1:
                        pe.wait_ge(q_sb, 1)
                    if b == 2:
                        pe.wait_ge(k_sb, 1)
                    if b == 3:
                        pe.wait_ge(vwf_sb, 1)
                    pe.matmul(bk[0:NK + 1, :], ct[0:DV + 1, b, :], wvf[0:DV + 1, :], start=True, stop=True).then_inc(vwf_ps, 1)

            def scores(m, g, b0):
                for b in (b0, b0 + 1):
                    if b == 0:
                        pe.wait_ge(vwf_sb, 2)
                    if b == 1:
                        pe.wait_ge(vwf_sb, 3)
                    if b >= 2:
                        pe.wait_ge(sc_sb, b - 1)
                    pe.matmul((XA, XB)[b % 2][:, 0:H * NK], qt[:, b * S:(b + 1) * S],
                              kblk[:, b, :, :].rearrange("p h k -> p (h k)"), start=True, stop=True).then_inc(sc_ps, 1)

            def attn_turn(m, g):
                pe.wait_ge(attn_ready, 1)
                for b in range(G):
                    t = pe.transpose(XA[0:NK + 1, b * S:(b + 1) * S], attn[:, b, :], ident[:, :])
                t.then_inc(at_ps, 1)

            def film_(m, g):
                pe.wait_ge(at_sb, 1)
                pe.wait_ge(vwf_sb, 4)
                for b in range(G):
                    if b >= 2:
                        pe.wait_ge(film_sb, b - 1)
                    pe.matmul((XB, XC)[b % 2][:, :], attnt[0:NK + 1, b * S:(b + 1) * S], vwf[0:NK + 1, b, :],
                              start=True, stop=True).then_inc(film_ps, 1)

            def conv_a(m, g):
                pe.wait_ge(xm_ready, 1)
                pe.wait_ge(film_sb, 4)
                for k, bk in enumerate((XA, XB)):
                    pe.matmul(bk[:, :], dft[:, k, :], qt[:, :], start=True, stop=True).then_inc(spec_ps, 1)

            def conv_c(m, g):
                pe.wait_ge(spec_ready, 2)
                pe.matmul(XC[:, :], dft[:, 2, :], spec[:, 0, :], start=True, stop=False)
                pe.matmul(XC[:, :], dft[:, 3, :], spec[:, 2, :], start=False, stop=True).then_inc(y_ps, 1)

            def ht_turn(m, g):
                pe.wait_ge(hh_ready, 1)
                for b in range(G):
                    t = pe.transpose(XA[:, b * S:(b + 1) * S], hh[:, b, :], ident[:, :])
                t.then_inc(ht_ps, 1)

            def xmlp_a(m, g):
                pe.wait_ge(ht_sb, 1)
                for c in range(HC):
                    if c == 3:
                        pe.wait_ge(gx_done, 1)
                    pe.matmul((XB, XC, XA, XB)[c][:, :], xw1[:, c * P:(c + 1) * P], ht[:, :], start=True, stop=True)\
                      .then_inc(xh_ps, 1)

            def xmlp_b(m, g):
                pe.wait_ge(gx_done, HC)
                for b in range(G):
                    for c in range(HC):
                        t = pe.matmul(XC[:, b * D:(b + 1) * D], gx[:, c, b * S:(b + 1) * S], xw2[:, c, :],
                                      start=(c == 0), stop=(c == HC - 1))
                t.then_inc(xo_ps, 1)

            def xt_turn(m, g):
                for k, (bk, src) in enumerate(((XA, hh), (XB, xh))):
                    pe.wait_ge(xf_ready, k + 1)
                    for b in range(G):
                        t = pe.transpose(bk[:, b * S:(b + 1) * S], src[:, b, :], ident[:, :])
                    t.then_inc(xft_ps, 1)

            def v_free():
                if n["wb"]:
                    pe.wait_ge(wb_sb, n["wb"])
                if n["hidden"]:
                    pe.wait_ge(mg_done, n["hidden"])
                if n["h1"]:
                    pe.wait_ge(h1_ready, 2 * n["h1"])

            def gate_a(g, m):
                for b in range(G):
                    t = pe.matmul(V[:, b * NX:(b + 1) * NX], xft[:, b * S:(b + 1) * S], gatew[:, :], start=True, stop=True)
                t.then_inc(gl_ps, 1)

            def gate_d(g, m):
                pe.wait_ge(wp_ready, 1)
                hb = HA[0:3 * NX, 0:GT // 2].bitcast(BF16)
                for b in range(G):
                    t = pe.transpose(hb[:, b * S:(b + 1) * S], wp[:, b, :, :].rearrange("p k e -> p (k e)"), identb[:, :])
                t.then_inc(wt_ps, 1)

            def wb(g, m, i):
                pe.wait_ge(wt_sb, 1)
                v_free()
                pe.matmul(V[:, :], esel[:, OUTS[i], :], wt[:, :], start=True, stop=True).then_inc(wb_ps, 1)
                n["wb"] += 1

            def use(g, m):
                for c in range(n["used"], n["used"] + STEP):
                    e, layer, k = CHUNKS[c]
                    if k == 0 and layer == 0 and e > 0:
                        pe.wait_ge(zc_ready, 2 * e)
                    if k == 0 and layer == 1 and n["out"]:
                        pe.wait_ge(part_ready, n["out"])
                    pe.wait_ge(basis_ready, c + 1)
                    if layer == 0:
                        for h in range(2):
                            t = pe.matmul(Z[h][:, :], kw0[:, e, k, h * P:(h + 1) * P], ring[:, c % RING, :],
                                          start=(k == 0), stop=(k == NG - 1))
                    else:
                        t = pe.matmul(O[:, :], kw1[:, e, k, :], ring[:, c % RING, :], start=(k == 0), stop=(k == 2 * NG - 1))
                        if k == 2 * NG - 1:
                            n["out"] += 1
                    t.then_inc(basis_used, 1)
                n["used"] += STEP

            def mlp(g, m, e):
                def hidden(c):
                    if c == 0:
                        if e == 0:
                            pe.wait_ge(wt_sb, 1)
                        else:
                            pe.wait_ge(mg_done, HC * e)
                    if c == 1:
                        v_free()
                    if c >= 2:
                        pe.wait_ge(mg_done, HC * e + c - 1)
                    pe.matmul((HA, V)[c % 2][:, :], mw1[:, e, c * P:(c + 1) * P], xft[:, :], start=True, stop=True)\
                      .then_inc(mh_ps, 1)

                def output(c):
                    if c == 0 and n["out"]:
                        pe.wait_ge(part_ready, n["out"])
                    pe.wait_ge(mg_done, HC * e + c + 1)
                    pe.matmul(O[:, :], mw2[:, e, c, :], mg[:, c % 2, :], start=(c == 0), stop=(c == HC - 1)).then_inc(mg_used, 1)

                hidden(0)
                hidden(1)
                for c in range(HC):
                    output(c)
                    if c + 2 < HC:
                        hidden(c + 2)
                n["hidden"] += HC
                n["out"] += 1

            def var_a(g, m, e):
                pe.wait_ge(zq_ready, 2 * e + 2)
                v_free()
                for b in range(G):
                    for h in range(2):
                        t = pe.matmul(V[:, b:b + 1], zq[:, h, b * S:(b + 1) * S], mean_w[:, 0:1], start=(h == 0), stop=(h == 1))
                t.then_inc(var_ps, 1)

            def var_b(g, m, e):
                pe.wait_ge(dg_ready, e + 1)
                pe.matmul(V[:, :], ones[:, :], dg[:, :, :].rearrange("p b t -> p (b t)"), start=True, stop=True).then_inc(rb_ps, 1)
                n["h1"] += 1

            def finish(g, m):
                pe.wait_ge(acc_ready, NX)
                for b in range(G):
                    t = pe.transpose(O[:, b * D:(b + 1) * D], acc[:, b * S:(b + 1) * S], ident[:, :])
                t.then_inc(yt_ps, 1)

            steps = dict(qk_turn=qk_turn, qk=qk, vwf=vwf_, scores=scores, attn_turn=attn_turn, film=film_, conv_a=conv_a,
                         conv_c=conv_c, ht_turn=ht_turn, xmlp_a=xmlp_a, xmlp_b=xmlp_b, xt_turn=xt_turn, gate_a=gate_a,
                         gate_d=gate_d, wb=wb, use=use, mlp=mlp, var_a=var_a, var_b=var_b, finish=finish)
            rounds(pe, "tensor", steps, n)

        @block.scalar
        def _(act):
            n = {}

            def copy(dst, src):
                return act.activation(dst, src, ACT.Copy)

            act.wait_ge(r_ready, 1)
            act.activation(tiny[:, 4:5], tiny[:, 3:4], ACT.Tanh, scale=0.5).then_inc(tanh_r, 1)
            act.wait_ge(in_film, 160)
            act.activation(gtanh[:, :], gates[:, 1:3], ACT.Tanh).then_inc(gates_tanh, 1)
            act.wait_ge(dt_args, 1)
            act.activation(s4t[:, 3, :], s4t[:, 0, :], ACT.Tanh, scale=0.5).then_inc(tanh_ar, 1)
            act.wait_ge(vec_ps, 1)
            copy(cols[:, :], XA[:, 0:NROWS]).then_inc(vec_sb, 1)
            act.wait_ge(wv_ps, 1)
            copy(wvt[:, 0:DV], XB[:, 0:DV]).then_inc(wv_sb, 1)
            act.wait_ge(tm_ps, 1)
            copy(tmt[:, :], HA[:, 0:NROW]).then_inc(wv_sb, 1)
            act.wait_ge(half_args, 2)
            act.activation(s4t[:, 5, :], s4t[:, 4, :], ACT.Sin, scale=TWO_PI).then_inc(sin_half, 1)
            act.activation(s4t[:, 7, :], s4t[:, 6, :], ACT.Sin, scale=TWO_PI).then_inc(sin_half, 1)
            act.wait_ge(stack_ps, 1)
            copy(acc[:, :], XC[:, :]).then_inc(stack_sb, 1)
            act.wait_ge(stack_sb, 1)
            for b in range(NB):
                t = act.activation(pw_e[:, b, :], stk[:, 0, :], ACT.Exp, scale=float(b))
            t.then_inc(fine_exp, 1)
            for i in range(NA):
                t = act.activation(pw_a[:, i, :], stk[:, 0, :], ACT.Exp, scale=float(NB * i))
            t.then_inc(coarse_exp, 1)
            act.wait_ge(fine_args, 1)
            act.activation(pw_r, pw_r, ACT.Sin, scale=TWO_PI).then_inc(fine_sin, 1)
            act.wait_ge(coarse_args, 1)
            act.activation(pw_cs, pw_cs, ACT.Sin, scale=TWO_PI).then_inc(coarse_sin, 1)
            act.wait_ge(wvf_ps, 1)
            copy(wvf[0:DV + 1, :], O[0:DV + 1, :])
            act.wait_ge(fine_pow, 1)
            act.wait_ge(coarse_pow, 1)
            for q, bk in enumerate((Z[0], Z[1], HA, V)):
                act.wait_ge(k_taps_ps, q + 1)
                copy(ka[:, :, 32 * q:32 * q + 32], bk[0:NA, :].rearrange("p (d b) -> p b d", b=NB)).then_inc(k_taps_sb, 1)
            act.wait_ge(kf_ps, 1)
            copy(kf[:, :, :].rearrange("p k d -> p (k d)"), XB[:, 0:2 * D])

            def qk_turn(m, g):
                act.wait_ge(x0t_ps, 1)
                copy(x0t[:, :], XA[:, :]).then_inc(x0t_sb, 1)
                act.wait_ge(ct_ps, 1)
                copy(ct[0:DV, :, 0:NK], XB[0:DV, 0:G * NK].rearrange("p (b k) -> p b k", b=G)).then_inc(ct_sb, 1)

            def qk(m, g):
                act.wait_ge(q_ps, 1)
                copy(qt[:, :], XA[:, :]).then_inc(q_sb, 1)

            def vwf_(m, g):
                for b, bk in enumerate((XC, XA, XB, XC)):
                    act.wait_ge(vwf_ps, b + 1)
                    copy(vwf[0:NK + 1, b, :], bk[0:NK + 1, :]).then_inc(vwf_sb, 1)

            def probs_b(m, g):
                act.wait_ge(diff_ready, 1)
                act.activation(scr[:, :, :, :], scr[:, :, :, :], ACT.Exp, scale=SCALE).then_inc(exp_ready, 1)

            def attn_turn(m, g):
                act.wait_ge(at_ps, 1)
                copy(attnt[0:NK + 1, :], XA[0:NK + 1, :]).then_inc(at_sb, 1)

            def film_(m, g):
                for b in range(G):
                    act.wait_ge(film_ps, b + 1)
                    copy(film[:, b, :], (XB, XC)[b % 2][:, :]).then_inc(film_sb, 1)

            def ht_turn(m, g):
                act.wait_ge(ht_ps, 1)
                copy(ht[:, :], XA[:, :]).then_inc(ht_sb, 1)

            def xmlp_a(m, g):
                for c in range(HC):
                    act.wait_ge(xh_ps, c + 1)
                    act.activation(gx[:, c, :], (XB, XC, XA, XB)[c][:, :], ACT.Gelu, bias=xb1[:, c:c + 1]).then_inc(gx_done, 1)

            def xt_turn(m, g):
                if m is not None:
                    act.wait_ge(tanh_done, len(CHUNKS))
                for k, (dst, bk) in enumerate(((xft, XA), (xkt, XB))):
                    act.wait_ge(xft_ps, k + 1)
                    copy(dst[:, :], bk[:, :]).then_inc(xt_turned, 1)

            def gate_b(g, m):
                act.wait_ge(gdiff, 1)
                act.activation(gs[:, 1, :], gs[:, 0, :], ACT.Exp).then_inc(gexp, 1)

            def wb(g, m, i):
                act.wait_ge(wb_ps, i + 1)
                if i >= 3:
                    act.wait_ge(part_ready, i - 2)
                copy(wbs[:, i % 3, :], V[:, :]).then_inc(wb_sb, 1)

            def make(g, m):
                for c in range(n["made"], n["made"] + STEP):
                    e, layer, k = CHUNKS[c]
                    if c >= RING:
                        act.wait_ge(basis_used, c - RING + 1)
                    if layer == 0:
                        src, sc, bi = xkt[:, :], scale0[:, e:e + 1], bias0[:, e, k:k + 1]
                    else:
                        h = k // NG
                        if k == 0:
                            act.wait_ge(h1_ready, 2 * e + 2)
                        src, sc, bi = h1[:, e % 2, h, :], scale1[:, 2 * e + h:2 * e + h + 1], bias1[:, 2 * e + h, k % NG:k % NG + 1]
                    act.activation(ring[:, c % RING, :], src, ACT.Tanh, bias=bi, scale=sc).then_inc(tanh_done, 1)
                n["made"] += STEP

            def mlp(g, m, e):
                b1 = ROW_OF["L0_ffn_mlp_b1"] + HC * e
                for c in range(HC):
                    act.wait_ge(mh_ps, HC * e + c + 1)
                    if HC * e + c >= 2:
                        act.wait_ge(mg_used, HC * e + c - 1)
                    act.activation(mg[:, c % 2, :], (HA, V)[c % 2][:, :], ACT.Gelu, bias=cols[:, b1 + c:b1 + c + 1])\
                       .then_inc(mg_done, 1)

            steps = dict(qk_turn=qk_turn, qk=qk, vwf=vwf_, probs_b=probs_b, attn_turn=attn_turn, film=film_, ht_turn=ht_turn,
                         xmlp_a=xmlp_a, xt_turn=xt_turn, gate_b=gate_b, wb=wb, make=make, mlp=mlp)
            rounds(act, "scalar", steps, n)

        @block.gpsimd
        def _(pool):
            n = {}

            pool.memset(ones[:, :], 1.0).then_inc(ones_made, 1)
            pool.memset(mean_w[:, :], 1.0 / F2).then_inc(ones_made, 1)
            pool.memset(minus_half[:, :], -0.5).then_inc(ones_made, 1)
            pool.memset(kblk[:, :, :, :], 0.0)
            pool.memset(attn[:, :, :], 1.0)
            pool.memset(ct[:, :, :], 0.0).then_inc(set_pool, 1)
            pool.wait_ge(set_pool, 1)
            pool.memset(ct[DV:DV + 1, :, NK:NK + 1], 1.0).then_inc(set_pool, 1)
            pool.wait_ge(set_pool, 2)
            for e in range(NE):
                pool.wait_ge(row_sums, e + 1)
                pool.tensor_tensor(kw0[:, e, :, :], kw0[:, e, :, :], rsum[:, e, :].unsqueeze(2).broadcast_to([P, NG, F2]),
                                   ALU.subtract).then_inc(centred, 1)

            def link(ins):
                n["own"] += 1
                ins.then_inc(pool_own, 1)
                pool.wait_ge(pool_own, n["own"])

            def ln_scale(q, twice):
                pool.wait_ge(ln_stats, q + 1)
                t, r, v, rr = (sml[:, 4 * q + k, :] for k in range(4))
                var = mv[:, :, 1]
                link(pool.tensor_scalar(t, var, EPS, None, ALU.add))
                ins = pool.tensor_tensor(r, t, minus_half[:, :], ALU.pow)
                if twice:
                    link(ins)
                    link(pool.tensor_tensor(v, var, r, ALU.mult))
                    link(pool.tensor_tensor(v, v, r, ALU.mult))
                    link(pool.tensor_scalar(v, v, EPS, None, ALU.add))
                    link(pool.tensor_tensor(t, v, minus_half[:, :], ALU.pow))
                    ins = pool.tensor_tensor(rr, r, t, ALU.mult)
                ins.then_inc(ln_scales, 1)

            def probs_a(m, g):
                pool.wait_ge(guard_ready, 1)
                s3 = scr[:, :, :, :].rearrange("p b h k -> p (b h) k")
                pool.tensor_tensor(s3, s3, sm16[:, 0, :].unsqueeze(2).broadcast_to([P, G * H, NK]), ALU.subtract)\
                    .then_inc(diff_ready, 1)

            def probs_c(m, g):
                pool.wait_ge(recip_ready, 1)
                s3 = scr[:, :, :, :].rearrange("p b h k -> p (b h) k")
                pool.tensor_tensor(s3, s3, sm16[:, 3, :].unsqueeze(2).broadcast_to([P, G * H, NK]), ALU.mult)\
                    .then_inc(prob_ready, 1)

            def modulate(m, g):
                pool.wait_ge(film_sb, 4)
                pool.tensor_tensor(x0[:, :, :], x0[:, :, :], film[:, :, 3 * D:4 * D], ALU.add).then_inc(xd_ready, 1)

            def conv_b(m, g):
                pool.wait_ge(spec_mul, 2)
                pool.tensor_tensor(spec[:, 0, :], spec[:, 0, :], spec[:, 1, :], ALU.subtract).then_inc(spec_ready, 1)
                pool.wait_ge(spec_mul, 4)
                pool.tensor_tensor(spec[:, 2, :], spec[:, 2, :], spec[:, 3, :], ALU.add).then_inc(spec_ready, 1)

            def conv_d(m, g):
                pool.wait_ge(y_mod, 1)
                pool.wait_ge(xd_ready, 1)
                pool.tensor_tensor(xt[:, :, :], xm, xt[:, :, :], ALU.add).then_inc(xt_ready, 1)

            def xmlp_b(m, g):
                pool.wait_ge(xo_add, 1)
                pool.tensor_tensor(xt[:, :, :], xt[:, :, :], b2row[:, :].unsqueeze(1).broadcast_to([P, G, D]), ALU.add)\
                    .then_inc(xt2_ready, 1)

            def ln3_out(m, g):
                pool.wait_ge(n_ready, 1)
                if m is not None:
                    pool.wait_ge(res_ready, 1)
                link(pool.tensor_tensor(xnew[:, :, :], hh, gout[:, :].unsqueeze(1).broadcast_to([P, G, D]), ALU.mult))
                link(pool.tensor_tensor(xnew[:, :, :], xnew[:, :, :], bout[:, :].unsqueeze(1).broadcast_to([P, G, D]), ALU.add))
                pool.tensor_tensor(xnew[:, :, :], xnew[:, :, :], xg[:, :, :], ALU.add).then_inc(xnew_ready, 1)

            def start(g, m):
                pool.tensor_copy(xres[:, :, :], xnew[:, :, :]).then_inc(res_ready, 1)

            def z_out(g, m, e):
                for h in range(2):
                    pool.wait_ge(zc_ready, 2 * e + h + 1)
                    pool.tensor_tensor(zq[:, h, :], zc[:, h, :], zc[:, h, :], ALU.mult).then_inc(zq_ready, 1)

            def var_a(g, m, e):
                pool.wait_ge(var_sb, e + 1)
                pool.tensor_tensor(vv[:, 1, :], vv[:, 0, :], minus_half[:, :], ALU.pow).then_inc(rstd_ready, 1)

            def comb(g, m, i):
                pool.wait_ge(part_ready, i + 1)
                if i == 0:
                    pool.tensor_copy(acc[:, :], part[:, 0, :]).then_inc(acc_ready, 1)
                    return
                pool.wait_ge(acc_ready, i)
                pool.tensor_tensor(acc[:, :], acc[:, :], part[:, i % 2, :], ALU.subtract if OUTS[i] >= NE else ALU.add)\
                    .then_inc(acc_ready, 1)

            steps = dict(ln1=lambda m, g: ln_scale(0, True), ln2=lambda m, g: ln_scale(1, False),
                         ln3=lambda m, g: ln_scale(2, False), ln4=lambda m, g: ln_scale(3, True),
                         probs_a=probs_a, probs_c=probs_c, modulate=modulate, conv_b=conv_b, conv_d=conv_d,
                         xmlp_b=xmlp_b, ln3_out=ln3_out, start=start, z_out=z_out, var_a=var_a, comb=comb)
            rounds(pool, "gpsimd", steps, n)

        @block.vector
        def _(dve):
            n = {}
            done = [0]
            chain = sem("set_chain")

            def step(ins):
                done[0] += 1
                ins.then_inc(chain, 1)
                dve.wait_ge(chain, done[0])

            ts, tt = dve.tensor_scalar, dve.tensor_tensor

            dve.wait_ge(in_s4, 96)
            c = [tiny[:, k:k + 1] for k in range(10)]
            step(ts(c[1], c[0], LOG2E, None, ALU.mult))
            step(ts(c[1], c[1], ROUND, ROUND, ALU.add, ALU.subtract))
            step(ts(c[2], c[1], -LN2_HI, None, ALU.mult))
            step(tt(c[2], c[0], c[2], ALU.add))
            step(ts(c[3], c[1], -LN2_LO, None, ALU.mult))
            step(tt(c[3], c[2], c[3], ALU.add))
            ts(tiny_i[:, :], c[1], 127.0, 8388608.0, ALU.add, ALU.mult).then_inc(r_ready, 1)
            dve.wait_ge(in_film, 160)
            gate = gates[:, 0:1]
            step(ts(wfilm, wfilm, gate, None, ALU.mult))
            step(ts(brow, brow, gates[0:1, 0:1], None, ALU.mult))
            step(ts(brow[:, 0:D], brow[:, 0:D], 1.0, None, ALU.add))
            step(ts(brow[:, 2 * D:3 * D], brow[:, 2 * D:3 * D], 1.0, None, ALU.add))
            for w, o, k in ((wfilm, wfs, P), (brow, brow2, 1)):
                step(tt(o[:, 0:D], w[:, 0:D], gnin[0:k, :], ALU.mult))
                step(tt(o[:, D:2 * D], w[:, 0:D], bnin[0:k, :], ALU.mult))
                step(tt(o[:, D:2 * D], o[:, D:2 * D], w[:, D:2 * D], ALU.add))
                ts(o[:, 2 * D:4 * D], w[:, 2 * D:4 * D], 1.0, None, ALU.mult).then_inc(film_w, 1)
            step(dve.memset(onehot, 0.0))
            step(dve.memset(wvt[:, DV:DV + 1], 0.0))
            dve.memset(onehot[:, DV:DV + 1], 1.0).then_inc(film_w, 1)
            dve.wait_ge(in_attn, 48)
            dve.tensor_copy(tm_rows, tm_u8).then_inc(tm_made, 1)
            dve.wait_ge(tanh_r, 1)
            step(ts(c[5], c[4], -1.0, 1.0, ALU.mult, ALU.add))
            step(ts(c[6], c[4], 1.0, None, ALU.add))
            step(dve.reciprocal(c[7], c[5]))
            step(tt(c[6], c[6], c[7], ALU.mult))
            step(tt(c[8], c[6], tiny_i[:, :].bitcast(F32), ALU.mult))
            dt = c[8]
            q = [s4t[:, k, :] for k in range(20)]
            a_re, a_im, c_re, c_im = (s4in[:, k, :] for k in range(4))
            step(ts(q[1], a_im, dt, 1.0 / (4 * np.pi), ALU.mult, ALU.mult))
            ts(q[0], a_re, dt, None, ALU.mult).then_inc(dt_args, 1)
            step(ts(q[2], q[1], ROUND, ROUND, ALU.add, ALU.subtract))
            tt(q[4], q[1], q[2], ALU.subtract).then_inc(half_args, 1)
            step(ts(q[8], q[1], 0.25, None, ALU.add))
            step(ts(q[9], q[8], ROUND, ROUND, ALU.add, ALU.subtract))
            tt(q[6], q[8], q[9], ALU.subtract).then_inc(half_args, 1)
            step(ts(q[10], q[1], 2.0, None, ALU.mult))
            step(ts(q[11], q[10], ROUND, ROUND, ALU.add, ALU.subtract))
            step(tt(q[10], q[10], q[11], ALU.subtract))
            step(tt(q[12], a_re, a_re, ALU.mult))
            step(tt(q[13], a_im, a_im, ALU.mult))
            step(tt(q[12], q[12], q[13], ALU.add))
            step(dve.reciprocal(q[13], q[12]))
            step(tt(q[14], c_re, a_re, ALU.mult))
            step(tt(q[15], c_im, a_im, ALU.mult))
            step(tt(q[14], q[14], q[15], ALU.add))
            step(tt(q[14], q[14], q[13], ALU.mult))
            step(tt(q[15], c_im, a_re, ALU.mult))
            step(tt(q[16], c_re, a_im, ALU.mult))
            step(tt(q[15], q[15], q[16], ALU.subtract))
            step(tt(q[15], q[15], q[13], ALU.mult))
            dve.wait_ge(tanh_ar, 1)
            step(ts(q[12], q[3], -1.0, 1.0, ALU.mult, ALU.add))
            step(dve.reciprocal(q[13], q[12]))
            step(tt(q[12], q[3], q[13], ALU.mult))
            step(ts(q[12], q[12], 2.0, None, ALU.mult))
            dve.wait_ge(sin_half, 2)
            step(tt(q[13], q[5], q[5], ALU.mult))
            step(ts(q[13], q[13], 2.0, None, ALU.mult))
            step(ts(q[16], q[13], -1.0, 1.0, ALU.mult, ALU.add))
            step(tt(q[16], q[16], q[12], ALU.mult))
            step(tt(q[16], q[16], q[13], ALU.subtract))
            step(tt(q[17], q[5], q[7], ALU.mult))
            step(ts(q[18], q[12], 1.0, 2.0, ALU.add, ALU.mult))
            step(tt(q[17], q[17], q[18], ALU.mult))
            step(tt(q[12], q[16], q[14], ALU.mult))
            step(tt(q[13], q[17], q[15], ALU.mult))
            step(tt(q[12], q[12], q[13], ALU.subtract))
            step(tt(q[13], q[16], q[15], ALU.mult))
            step(tt(q[18], q[17], q[14], ALU.mult))
            step(tt(q[13], q[13], q[18], ALU.add))
            for h in range(2):
                lo, hi = h * NST, (h + 1) * NST
                dve.tensor_copy(stack_d[:, 0, lo:hi], q[0])
                dve.tensor_copy(stack_d[:, 1, lo:hi], q[10])
                ts(stack_d[:, 2, lo:hi], q[12 + h], 2.0 - 4.0 * h, None, ALU.mult).then_inc(stack_made, 1)
                ts(stack_d[:, 3, lo:hi], q[13 - h], -2.0, None, ALU.mult).then_inc(stack_made, 1)
            dve.wait_ge(in_const, 64)
            dve.wait_ge(vec_sb, 1)
            dve.tensor_copy(identb[:, :], ident[:, :])
            dve.tensor_copy(esel[:, :, :], esel_in).then_inc(set_dve, 1)
            dve.wait_ge(b1_ps, 1)
            r = ROW_OF["L0_xattn_b1"]
            tt(xb1[:, :], V[:, 0:HC], cols[:, r:r + HC], ALU.add).then_inc(set_dve, 1)
            r = ROW_OF["L0_xattn_g_ffn"]
            ts(xw1[:, :], xw1[:, :], cols[:, r:r + 1], None, ALU.mult).then_inc(set_dve, 1)
            dve.wait_ge(gates_tanh, 1)
            ts(gout[:, :], gout[:, :], gtanh[:, 0:1], None, ALU.mult)
            ts(bout[:, :], bout[:, :], gtanh[:, 0:1], None, ALU.mult)
            dve.wait_ge(stack_sb, 1)
            for b in range(NB):
                t = ts(pw_r[:, b, :], stk[:, 1, :], float(b), misc[:, 0:1], ALU.mult, ALU.add)
            step(t)
            rr = rounded.rearrange("p (n d) -> p n d", n=NB)
            step(ts(rr, pw_r, ROUND, ROUND, ALU.add, ALU.subtract))
            tt(pw_r, pw_r, rr, ALU.subtract).then_inc(fine_args, 1)
            dve.wait_ge(fine_args, 1)
            for i in range(NA):
                ts(pw_cs[:, 0, i, :], stk[:, 1, :], float(NB * i), 0.25, ALU.mult, ALU.add)
                t = ts(pw_cs[:, 1, i, :], stk[:, 1, :], float(NB * i), None, ALU.mult)
            step(t)
            rc = rounded.rearrange("p (c n d) -> p c n d", c=2, n=NA)
            step(ts(rc, pw_cs, ROUND, ROUND, ALU.add, ALU.subtract))
            tt(pw_cs, pw_cs, rc, ALU.subtract).then_inc(coarse_args, 1)
            dve.wait_ge(fine_sin, 1)
            dve.wait_ge(fine_exp, 1)
            tt(pw_r, pw_r, pw_e, ALU.mult).then_inc(fine_pow, 1)
            dve.wait_ge(coarse_sin, 1)
            dve.wait_ge(coarse_exp, 1)
            step(tt(pw_cs[:, 0], pw_cs[:, 0], stk[:, 2:3, :].broadcast_to([P, NA, D]), ALU.mult))
            step(tt(pw_cs[:, 1], pw_cs[:, 1], stk[:, 3:4, :].broadcast_to([P, NA, D]), ALU.mult))
            step(tt(pw_cs[:, 0], pw_cs[:, 0], pw_cs[:, 1], ALU.add))
            tt(pw_a, pw_a, pw_cs[:, 0], ALU.mult).then_inc(coarse_pow, 1)
            grid = misc[:, 9:17]
            for g_, b_, sc_, bi_, k in (("L0_ffn_kan_ln_g0", "L0_ffn_kan_ln_b0", scale0, bias0, NE),
                                        ("L0_ffn_kan_ln_g1", "L0_ffn_kan_ln_b1", scale1, bias1, 2 * NE)):
                ts(sc_[:, :], cols[:, ROW_OF[g_]:ROW_OF[g_] + k], 0.5, None, ALU.mult)
                step(ts(cols[:, ROW_OF[b_]:ROW_OF[b_] + k], cols[:, ROW_OF[b_]:ROW_OF[b_] + k], 0.5, None, ALU.mult))
                tt(bi_[:, :, :], cols[:, ROW_OF[b_]:ROW_OF[b_] + k].unsqueeze(2).broadcast_to([P, k, NG]),
                   grid.unsqueeze(1).broadcast_to([P, k, NG]), ALU.add)
            for e in range(NE):
                dve.wait_ge(in_kw0[e], 16)
                step(dve.tensor_reduce(rsum[:, e, :], kw0[:, e, :, :], AX.X, ALU.add))
                ts(rsum[:, e, :], rsum[:, e, :], 1.0 / F2, None, ALU.mult).then_inc(row_sums, 1)
            dve.wait_ge(const_ps, 1)
            r = ROW_OF["L0_ffn_kan_sl_b0"]
            step(tt(const0[:, :, :].rearrange("p e h -> p (e h)"), XA[:, 0:2 * NE], cols[:, r:r + 2 * NE], ALU.add))
            tt(const0[:, :, :], const0[:, :, :], XA[:, 3 * NE:4 * NE].unsqueeze(2).broadcast_to([P, NE, 2]), ALU.subtract)
            r = ROW_OF["L0_ffn_kan_sl_b1"]
            tt(const1[:, :], XA[:, 2 * NE:3 * NE], cols[:, r:r + NE], ALU.add)

            def link(ins):
                n["own"] += 1
                ins.then_inc(dve_own, 1)
                dve.wait_ge(dve_own, n["own"])

            def stats(src):
                for b in range(G):
                    t = dve.bn_stats(st[:, b, :], src[:, b, :])
                link(t)
                for b in range(G):
                    t = dve.bn_aggr(mv[:, b, :], st[:, b, :])
                t.then_inc(ln_stats, 1)

            def normalise(dst, src, scale):
                for b in range(G):
                    t = ts(dst[:, b, :], src[:, b, :], mv[:, b, 0:1], sml[:, scale, b:b + 1], ALU.subtract, ALU.mult)
                return t

            def ln1(m, g):
                dve.wait_ge(x_in, 16)
                stats(xg)
                if isinstance(g, int):
                    dve.tensor_copy(tmg[:, :], tmt[:, g * G:(g + 1) * G])
                else:
                    dve.tensor_copy(tmg[:, :], tmt[:, bass.ds(g * G, G)])
                dve.wait_ge(vmask_in, 16)
                ts(vmb[:, :], vmu[:, :], BIG, BIG, ALU.mult, ALU.subtract)

            def ln1_out(m, g):
                dve.wait_ge(ln_scales, 1)
                normalise(x0, xg, 1).then_inc(x0_ready, 1)
                link(normalise(xh, xg, 3))

            def qk(m, g):
                dve.wait_ge(k_ps, 1)
                for h in range(H):
                    lo, hi = h * DH, (h + 1) * DH
                    t = dve.tensor_copy(kblk[lo:hi, :, h, :], XB[lo:hi, 0:G * NK].rearrange("p (b k) -> p b k", b=G))
                t.then_inc(k_sb, 1)

            def scores(m, g, b0):
                for b in (b0, b0 + 1):
                    dve.wait_ge(sc_ps, b + 1)
                    tt(scr[:, b, :, :], (XA, XB)[b % 2][:, 0:H * NK].rearrange("p (h k) -> p h k", h=H),
                       vmb[:, b * NK:(b + 1) * NK].unsqueeze(1).broadcast_to([P, H, NK]), ALU.add).then_inc(sc_sb, 1)

            def topk(m, g, b, r):
                if r == 0:
                    dve.wait_ge(sc_sb, b + 1)
                src = scr if r == 0 else left
                for h in range(H):
                    t = dve.max(top[:, b, h, min(r, 1), :], src[:, b, h, :])
                link(t)
                for h in range(H):
                    t = dve.match_replace(out=left[:, b, h, :], in_to_replace=top[:, b, h, min(r, 1), :],
                                          in_values=src[:, b, h, :], imm_value=TAKEN)
                link(t)

            def probs_a(m, g):
                ts(sm16[:, 0, :].rearrange("p (b h) -> p b h", b=G), top[:, :, :, 0, 0], GUARD, None, ALU.max)\
                    .then_inc(guard_ready, 1)

            def probs_c(m, g):
                dve.wait_ge(exp_ready, 1)
                s2 = scr[:, :, :, :].rearrange("p b h k -> p (b h k)")
                link(dve.scalar_tensor_tensor(out=s2, in0=left[:, :, :, :].rearrange("p b h k -> p (b h k)"), scalar=TAKEN,
                                              in1=s2, op0=ALU.is_equal, op1=ALU.mult))
                link(dve.tensor_reduce(sm16[:, 1, :], scr[:, :, :, :].rearrange("p b h k -> p (b h) k"), AX.X, ALU.add))
                link(dve.reciprocal(sm16[:, 2, :], sm16[:, 1, :]))
                dve.scalar_tensor_tensor(out=sm16[:, 3, :].rearrange("p (b h) -> p b h", b=G),
                                         in0=sm16[:, 2, :].rearrange("p (b h) -> p b h", b=G), scalar=1.0 / H,
                                         in1=tmg[:, :].unsqueeze(2).broadcast_to([P, G, H]), op0=ALU.mult, op1=ALU.mult)\
                   .then_inc(recip_ready, 1)

            def attn_turn(m, g):
                dve.wait_ge(prob_ready, 1)
                dve.tensor_reduce(attn[:, :, 0:NK], scr[:, :, :, :].rearrange("p b h k -> p b k h"), AX.X, ALU.add)\
                   .then_inc(attn_ready, 1)

            def modulate(m, g):
                dve.wait_ge(film_sb, 4)
                link(tt(xm, xh[:, :, :], film[:, :, 0:D], ALU.mult))
                tt(xm, xm, film[:, :, D:2 * D], ALU.add).then_inc(xm_ready, 1)

            def conv_b(m, g):
                for k, (bk, c_) in enumerate(((XA, 0), (XB, 1), (XA, 1), (XB, 0))):
                    dve.wait_ge(spec_ps, k % 2 + 1)
                    tt(spec[:, k, :].rearrange("p (b d) -> p b d", b=G), bk[:, :].rearrange("p (b d) -> p b d", b=G),
                       kf[:, c_:c_ + 1, :].broadcast_to([P, G, D]), ALU.mult).then_inc(spec_mul, 1)

            def conv_d(m, g):
                dve.wait_ge(y_ps, 1)
                tt(xm, XC[:, :].rearrange("p (b d) -> p b d", b=G), film[:, :, 2 * D:3 * D], ALU.mult).then_inc(y_mod, 1)

            def ln2(m, g):
                dve.wait_ge(xt_ready, 1)
                stats(xt)

            def ln2_out(m, g):
                dve.wait_ge(ln_scales, 2)
                normalise(hh, xt, 5).then_inc(hh_ready, 1)

            def xmlp_b(m, g):
                dve.wait_ge(xo_ps, 1)
                tt(xt[:, :, :], XC[:, :].rearrange("p (b d) -> p b d", b=G), xt[:, :, :], ALU.add).then_inc(xo_add, 1)

            def ln3(m, g):
                dve.wait_ge(xt2_ready, 1)
                stats(xt)

            def ln3_out(m, g):
                dve.wait_ge(ln_scales, 3)
                normalise(hh, xt, 9).then_inc(n_ready, 1)

            def ln4(m, g):
                dve.wait_ge(xnew_ready, 1)
                stats(xnew)

            def ln4_out(m, g):
                dve.wait_ge(ln_scales, 4)
                normalise(hh, xnew, 13).then_inc(xf_ready, 1)
                normalise(xh, xnew, 15).then_inc(xf_ready, 1)

            def make(g, m):
                for c_ in range(n["made"], n["made"] + STEP):
                    dve.wait_ge(tanh_done, c_ + 1)
                    tt(ring[:, c_ % RING, :], ring[:, c_ % RING, :], ring[:, c_ % RING, :], ALU.mult).then_inc(basis_ready, 1)
                n["made"] += STEP

            def gate_a(g, m):
                dve.wait_ge(gl_ps, 1)
                link(dve.tensor_copy(gl[:, :, :].rearrange("p b e -> p (b e)"), V[:, 0:G * NX]))
                for b in range(G):
                    t = dve.max(gtop[:, b, :], gl[:, b, :])
                link(t)
                for b in range(G):
                    dve.max_index(gidx[:, b, :], gtop[:, b, :], gl[:, b, :])
                tt(gs[:, 0, :], gtop[:, :, 1], gtop[:, :, 0], ALU.subtract).then_inc(gdiff, 1)

            def gate_c(g, m):
                dve.wait_ge(gexp, 1)
                e2, den, w1, w2 = (gs[:, k, :] for k in (1, 2, 3, 4))
                link(dve.tensor_copy(gidf[:, :, :], gidx[:, :, :]))
                link(ts(den, e2, 1.0, None, ALU.add))
                link(dve.reciprocal(w1, den))
                link(ts(w1, w1, gtanh[:, 1:2], None, ALU.mult))
                link(tt(w2, e2, w1, ALU.mult))
                iota = misc[:, 1:9].unsqueeze(1).broadcast_to([P, G, NX])
                for k, w in ((0, w1), (1, w2)):
                    link(tt(gw[:, k], iota, gidf[:, :, k:k + 1].broadcast_to([P, G, NX]), ALU.is_equal))
                    link(tt(gw[:, k], gw[:, k], w.unsqueeze(2).broadcast_to([P, G, NX]), ALU.mult))
                link(tt(gw[:, 2], gw[:, 0], gw[:, 1], ALU.add))
                link(dve.tensor_copy(wp[:, :, 0, :], gw[:, 2]))
                link(tt(gw[:, 3], gw[:, 2], wp[:, :, 0, :], ALU.subtract))
                link(dve.tensor_copy(wp[:, :, 1, :], gw[:, 3]))
                link(tt(gw[:, 4], gw[:, 3], wp[:, :, 1, :], ALU.subtract))
                dve.tensor_copy(wp[:, :, 2, :], gw[:, 4]).then_inc(wp_ready, 1)

            def gate_d(g, m):
                dve.wait_ge(wt_ps, 1)
                dve.tensor_copy(wt[:, :], HA[0:3 * NX, 0:GT // 2].bitcast(BF16)).then_inc(wt_sb, 1)

            def z_out(g, m, e):
                dve.wait_ge(basis_used, Z_DONE[e])
                if e > 0:
                    dve.wait_ge(h1_ready, 2 * e)
                for h in range(2):
                    ts(zc[:, h, :], Z[h][:, :], -1.0, const0[:, e, h:h + 1], ALU.mult, ALU.add).then_inc(zc_ready, 1)

            def var_a(g, m, e):
                dve.wait_ge(var_ps, e + 1)
                ts(vv[:, 0, :], V[:, 0:G], EPS, None, ALU.add).then_inc(var_sb, 1)

            def var_b(g, m, e):
                dve.wait_ge(rstd_ready, e + 1)
                tt(dg[:, :, :], ident[:, :].unsqueeze(1).broadcast_to([P, G, P]),
                   vv[:, 1, :].unsqueeze(2).broadcast_to([P, G, P]), ALU.mult).then_inc(dg_ready, 1)
                dve.wait_ge(rb_ps, e + 1)
                for h in range(2):
                    tt(h1[:, e % 2, h, :], zc[:, h, :], V[:, :], ALU.mult).then_inc(h1_ready, 1)

            def comb(g, m, i):
                x = OUTS[i]
                dve.wait_ge(*out_done(i))
                dve.wait_ge(wb_sb, i + 1)
                if i >= 2:
                    dve.wait_ge(acc_ready, i - 1)
                r = ROW_OF["L0_ffn_mlp_b2"] + x
                col, op = (cols[:, r:r + 1], ALU.add) if x < NE else (const1[:, x - NE:x - NE + 1], ALU.subtract)
                dve.scalar_tensor_tensor(out=part[:, i % 2, :], in0=O[:, :], scalar=col, in1=wbs[:, i % 3, :], op0=op,
                                         op1=ALU.mult).then_inc(part_ready, 1)

            def finish(g, m):
                dve.wait_ge(yt_ps, 1)
                dve.wait_ge(res_ready, 1)
                tt(yout, O[:, :].rearrange("p (b d) -> p b d", b=G), xres[:, :, :], ALU.add).then_inc(y_ready, 1)

            Z_DONE = [CHUNKS.index((e, 0, NG - 1)) + 1 for e in range(NE)]

            def out_done(i):
                x = OUTS[i]
                if x < NE:
                    return mg_used, HC * (x + 1)
                return basis_used, CHUNKS.index((x - NE, 1, 2 * NG - 1)) + 1

            steps = dict(ln1=ln1, ln1_out=ln1_out, qk=qk, scores=scores, topk=topk, probs_a=probs_a, probs_c=probs_c,
                         attn_turn=attn_turn, modulate=modulate, conv_b=conv_b, conv_d=conv_d, ln2=ln2, ln2_out=ln2_out,
                         xmlp_b=xmlp_b, ln3=ln3, ln3_out=ln3_out, ln4=ln4, ln4_out=ln4_out, make=make, gate_a=gate_a,
                         gate_c=gate_c, gate_d=gate_d, z_out=z_out, var_a=var_a, var_b=var_b, comb=comb, finish=finish)
            rounds(dve, "vector", steps, n)


def shape_constants():
    f, t = np.arange(P)[None, :], np.arange(S)[:, None]
    ang = np.pi * (2 * f + 1) * t / (2.0 * S)
    ang_i = ang.T
    dft = np.stack([np.cos(ang), -np.sin(ang), np.cos(ang_i) / S, -np.sin(ang_i) / S], axis=1)
    esel = np.zeros((3, NX, NX, P))
    for e in range(NX):
        esel[:, e, e, :] = 1.0
    misc = np.zeros((P, 17))
    misc[0:NST, 0] = 0.25
    misc[:, 1:9] = np.arange(NX)
    misc[:, 9:17] = -0.5 * np.linspace(-1.2, 0.2, NG).astype(np.float32)
    return {"c_dft": dft.astype(np.float32), "c_ident": np.eye(P, dtype=np.float32),
            "c_esel": esel.reshape(3 * NX, NX, P).astype(np.float32), "c_misc": misc.astype(np.float32)}


def kernel(**inputs):
    import concourse.bacc as _bacc
    from concourse.bass_utils import run_bass_kernel_spmd as _run

    nc = _bacc.Bacc("TRN2", target_bir_lowering=False, num_devices=1)
    names = {"mask_BxS_bf1": "mask_text", "mask_BxS2_bf1": "mask_vision"}
    arrays, aps = {}, {}
    for name, value in list(inputs.items()) + list(shape_constants().items()):
        v = np.ascontiguousarray(value)
        if v.dtype == np.bool_:
            v = v.view(np.uint8)
        if v.ndim == 0:
            v = v.reshape(1)
        name = names.get(name, name)
        arrays[f"in_{name}"] = v
        aps[name] = nc.dram_tensor(f"in_{name}", v.shape, mybir.dt.from_np(v.dtype), kind="ExternalInput").ap()
    out = nc.dram_tensor("out_0", tuple(inputs["x"].shape), F32, kind="ExternalOutput").ap()
    build(nc, aps, out)
    r = _run(nc, [arrays], core_ids=[0])
    return r.results[0]["out_0"]
```

```python
from contextlib import ExitStack

import numpy as np

import concourse.bass as bass
from concourse import mybir

F32 = mybir.dt.float32
BF16 = mybir.dt.bfloat16
U8 = mybir.dt.uint8
U32 = mybir.dt.uint32
I32 = mybir.dt.int32
ALU = mybir.AluOpType
ACT = mybir.ActivationFunctionType
AX = mybir.AxisListType

P = 128
S = 128
D = 128
G = 4
GT = G * S
NK = 77
DV = 96
H = 4
DH = 32
TOPK = 32
HID = 512
HC = HID // P
NE = 4
NX = 2 * NE
NG = 8
F2 = 256
NST = 64
NB = 16
NA = S // NB
EPS = 1e-5
SCALE = float(1.0 / np.sqrt(np.float32(DH)))
BIG = 1e30
GUARD = -1e29
TAKEN = -3.0e38
ROUND = 12582912.0
TWO_PI = 6.2831845
LOG2E, LN2_HI, LN2_LO = 1.4426950408889634, 0.693359375, -2.12194440e-4
RING = 8
STEP = 2

VECS = [("L0_ffn_kan_ln_g0", NE), ("L0_ffn_kan_ln_b0", NE), ("L0_ffn_kan_ln_g1", 2 * NE), ("L0_ffn_kan_ln_b1", 2 * NE),
        ("L0_ffn_kan_sl_b0", 2 * NE), ("L0_ffn_kan_sl_b1", NE), ("L0_ffn_mlp_b1", HC * NE), ("L0_ffn_mlp_b2", NE),
        ("L0_xattn_b1", HC), ("L0_xattn_g_ffn", 1), ("L0_xattn_b_ffn", 1)]
ROW_OF, _r = {}, 0
for _n, _k in VECS:
    ROW_OF[_n] = _r
    _r += _k
NROWS = _r

CHUNKS = [(e, layer, k) for e, layer in [(0, 0), (1, 0), (0, 1), (2, 0), (1, 1), (3, 0), (2, 1), (3, 1)]
          for k in range(NG * (layer + 1))]
OUTS = [0, 1, NE, 2, NE + 1, 3, NE + 2, NE + 3]


ATTENTION = ("load", "ln1", "ln1_out", "qk_turn", "qk", "vwf", "scores", "topk", "probs_a", "probs_b", "probs_c", "attn_sum",
             "attn_turn", "film", "modulate", "conv_a", "conv_b", "conv_c", "conv_d", "ln2", "ln2_out", "ht_turn",
             "xmlp_a", "xmlp_b", "ln3", "ln3_out", "ln4", "ln4_out", "xt_turn")

SCHEDULE = """
start tanh load tanh make gate_a ln1 tanh tanh make ln1_out make mlp_a:0 use tanh gate_b make use qk_turn tanh mlp_b:0
use mlp_c:0 qk vwf use mlp_a:1 make tanh make gate_c z_out:0 scores:0 scores:2 topk:0:0 topk:0:1 gate_d tanh make
topk:0:2 topk:0:3 var_a:0 topk:1:0 use use topk:1:1 var_b:0 var_c:0 wb:0 make comb:0 tanh make use topk:1:2 tanh
mlp_b:1 make tanh make mlp_c:1 topk:1:3 wb:1 use tanh comb:1 wb:2 use make use z_out:1 topk:2:0 topk:2:1 topk:2:2
topk:2:3 use tanh make var_a:1 use tanh tanh make use use make use topk:3:0 var_b:1 tanh tanh make make topk:3:1 tanh
topk:3:2 tanh make var_c:1 use use topk:3:3 wb:3 tanh use probs_a probs_b make comb:2 make use probs_c mlp_a:2 tanh
mlp_b:2 tanh attn_sum tanh mlp_c:2 attn_turn use film make comb:3 tanh make z_out:2 make use use use make tanh
modulate use tanh make tanh conv_a tanh conv_b make make make var_a:2 use conv_c wb:4 use tanh conv_d var_b:2 tanh ln2
use use make ln2_out comb:4 make ht_turn tanh use xmlp_a make mlp_a:3 var_c:2 xmlp_b tanh use ln3 tanh make mlp_b:3
mlp_c:3 wb:5 use ln3_out make use use tanh ln4 make tanh make comb:5 tanh z_out:3 make use use tanh make ln4_out tanh
var_a:3 tanh make use use var_b:3 tanh make var_c:3 use tanh wb:6 use make comb:6 use tanh xt_turn make tanh use tanh
make tanh use make tanh use make use wb:7 make make tanh tanh use use make make use use comb:7 finish
"""


SETUP = {
    ("load",): [("late_loads",), ("s4_dt",)],
    ("ln1",): [("s4_half",)],
    ("qk_turn",): [("s4_turn",)],
    ("vwf",): [("s4_exp",), ("s4_args",)],
    ("scores", 2): [("s4_pow",), ("s4_taps",)],
    ("topk", 2, 0): [("s4_spectrum",)],
    ("probs_b",): [("kan0", 0)],
    ("probs_c",): [("kan0", 1)],
    ("modulate",): [("kan1", 0)],
    ("conv_c",): [("kan0", 2)],
    ("ln2",): [("kan1", 1)],
    ("ht_turn",): [("kan0", 3)],
    ("xmlp_a",): [("kan1", 2), ("kan1", 3)],
    ("ln3",): [("kan_const",)],
    ("xt_turn",): [("late_loads_in",)],
}


def schedule():
    return [(w[0], *map(int, w[1:])) for w in (step.split(":") for step in SCHEDULE.split())]


def both_steps():
    return schedule()


def mixture_steps():
    return [s for s in both_steps() if s[0] not in ATTENTION]


def attention_steps():
    res = []
    for s in both_steps():
        if s[0] in ATTENTION:
            res += [s] + SETUP.get(s, [])
    return res


def build(nc, a, out):
    NROW = a["x"].shape[0]
    NGROUPS = NROW // G
    kscratch = nc.dram_tensor("k_scratch", (S, D), F32, kind="Internal").ap()

    with ExitStack() as ctx:
        def sb(name, shape, dt=F32):
            return ctx.enter_context(nc.sbuf_tensor(name, shape, dt))

        def bank(name):
            return ctx.enter_context(nc.psum_tensor(name, [P, GT], F32))

        def sem(name):
            return ctx.enter_context(nc.semaphore(name))

        kw0 = sb("kw0", [P, NE, NG, F2])
        kw1 = sb("kw1", [P, NE, 2 * NG, D])
        mw1 = sb("mw1", [P, NE, HID])
        mw2 = sb("mw2", [P, NE, HC, D])
        gatew = sb("gatew", [P, NX])
        wq = sb("wq", [P, P])
        wk = sb("wk", [P, P])
        wvf = sb("wvf", [P, 4 * D])
        xw1 = sb("xw1", [P, HID])
        xw2 = sb("xw2", [P, HC, D])
        dft = sb("dft", [P, 4, P])
        kf = sb("kf", [P, 2, D])
        ident = sb("ident", [P, P])
        identb = sb("identb", [P, P], BF16)
        ones = sb("ones", [P, P])
        mean_w = sb("mean_w", [P, P])
        esel = sb("esel", [3 * NX, NX, P], BF16)
        misc = sb("misc", [P, 17])
        cols = sb("cols", [P, NROWS])
        scale0 = sb("scale0", [P, NE])
        bias0 = sb("bias0", [P, NE, NG])
        scale1 = sb("scale1", [P, 2 * NE])
        bias1 = sb("bias1", [P, 2 * NE, NG])
        const0 = sb("const0", [P, NE, 2])
        const1 = sb("const1", [P, NE])
        xb1 = sb("xb1", [P, HC])
        gout = sb("gout", [P, D])
        bout = sb("bout", [P, D])
        b2row = sb("b2row", [P, D])
        tmt = sb("tmt", [P, NROW])
        gates = sb("gates", [P, 3])
        gtanh = sb("gtanh", [P, 2])
        minus_half = sb("minus_half", [P, G])
        xg = sb("xg", [P, G, D])
        cg = sb("cg", [NK, G, DV])
        vmu = sb("vmu", [P, G * NK], U8)
        vmb = sb("vmb", [P, G * NK])
        tmg = sb("tmg", [P, G])
        x0 = sb("x0", [P, G, D])
        xh = sb("xh", [P, G, D])
        x0t = sb("x0t", [P, GT])
        ct = sb("ct", [P, G, NK + 1])
        qt = sb("qt", [P, GT])
        kblk = sb("kblk", [P, G, H, NK])
        vwf = sb("vwf", [P, G, 4 * D])
        scr = sb("scr", [P, G, H, NK])
        left = sb("left", [P, G, H, NK])
        top = sb("top", [P, G, H, 2, 8])
        attn = sb("attn", [P, G, NK + 1])
        attnt = sb("attnt", [P, GT])
        film = sb("film", [P, G, 4 * D])
        xnew = sb("xnew", [P, G, D])
        st = sb("st", [P, G, 6])
        mv = sb("mv", [P, G, 2])
        sml = sb("sml", [P, 16, G])
        sm16 = sb("sm16", [P, 4, G * H])
        xft = sb("xft", [P, GT])
        xkt = sb("xkt", [P, GT])
        xres = sb("xres", [P, G, D])
        ring = sb("ring", [P, RING, GT])
        zc = sb("zc", [P, 2, GT])
        zq = sb("zq", [P, 2, GT])
        h1 = sb("h1", [P, 2, 2, GT])
        dg = sb("dg", [P, G, P])
        vv = sb("vv", [P, 2, G])
        mg = sb("mg", [P, 2, GT])
        wbs = sb("wbs", [P, 3, GT])
        part = sb("part", [P, 2, GT])
        acc = sb("acc", [P, GT])
        gl = sb("gl", [P, G, NX])
        gtop = sb("gtop", [P, G, 8])
        gidx = sb("gidx", [P, G, 8], U32)
        gidf = sb("gidf", [P, G, 8])
        gs = sb("gs", [P, 5, G])
        gw = sb("gw", [P, 5, G, NX])
        wp = sb("wp", [P, G, 3, NX], BF16)
        wt = sb("wt", [3 * NX, GT], BF16)
        xm = qt[:, :].rearrange("p (b d) -> p b d", b=G)
        hh = x0t[:, :].rearrange("p (b d) -> p b d", b=G)
        ht = attnt
        spec = vwf
        gx = vwf
        xt = x0
        yout = wbs[:, 0, :].rearrange("p (b d) -> p b d", b=G)
        pw_r = ring[:, 0:4, :].rearrange("p a b -> p (a b)").rearrange("p (n d) -> p n d", n=NB)
        pw_e = ring[:, 4:8, :].rearrange("p a b -> p (a b)").rearrange("p (n d) -> p n d", n=NB)
        pw_cs = film[:, :, :].rearrange("p a b -> p (a b)").rearrange("p (c n d) -> p c n d", c=2, n=NA)
        rounded = h1[:, :, :, :].rearrange("p a b c -> p (a b c)")
        pw_a = zc[:, :, :].rearrange("p a b -> p (a b)").rearrange("p (n d) -> p n d", n=NA)
        ka = h1[0:NA, :, :, :].rearrange("p a b c -> p (a b c)").rearrange("p (n d) -> p n d", n=NB)
        kl = zq[:, 0, 0:D]
        s4flat = ring[:, 0:4, :].rearrange("p a b -> p (a b)")
        stack_d = s4flat[:, 0:512].rearrange("p (k c) -> p k c", k=4)
        s4in = s4flat[:, 512:768].rearrange("p (k n) -> p k n", k=4)
        s4t = s4flat[:, 768:2048].rearrange("p (k n) -> p k n", n=NST)
        stk = acc[:, :].rearrange("p (k d) -> p k d", k=4)
        wfs = part[:, 0, :]
        wvin = part[:, 1, 0:D]
        wvt = part[:, 1, D:2 * D]
        wfilm = dg[:, :, :].rearrange("p a b -> p (a b)")
        gnin = xh[:, 0, :]
        bnin = xh[:, 1, :]
        vrows = xh[:, 2, :]
        tm_u8 = vmu[0:NROW, 0:S]
        tm_rows = xh[0:NROW, 3, :]
        sflat = scr[:, :, :, :].rearrange("p a b c -> p (a b c)")
        brow = sflat[0:1, 0:512]
        brow2 = sflat[0:1, 512:1024]
        lflat = left[:, :, :, :].rearrange("p a b c -> p (a b c)")
        drow = wbs[0:1, 1, 0:D]
        sum0 = mg[:, :, :].rearrange("p a b -> p (a b)").rearrange("p (e o) -> p e o", e=NE)
        sum1 = part[:, 0, :].rearrange("p (e o) -> p e o", e=NE)
        onehot = lflat[0:1, D:D + DV + 1]
        esel_in = mg[0:3 * NX, :, :].rearrange("p a b -> p (a b)").rearrange("p (k m) -> p k m", k=NX)
        tiny = gw[:, :, :, :].rearrange("p a b c -> p (a b c)")
        tiny_i = sb("tiny_i", [P, 1], I32)
        rsum = sb("rsum", [P, NE, NG])
        rsum_all = sb("rsum_all", [P, NE])

        Z = [bank("Z0"), bank("Z1")]
        HA, V, O, XA, XB, XC = bank("HA"), bank("V"), bank("O"), bank("XA"), bank("XB"), bank("XC")

        in_const, in_s4, in_attn, in_film, in_xmlp, in_vec, in_moe, in_kw1 = [
            sem("in_" + n) for n in ("const", "s4", "attn", "film", "xmlp", "vec", "moe", "kw1")]
        in_kw0 = [sem(f"in_kw0_{e}") for e in range(NE)]
        set_dve, set_pool = sem("set_dve"), sem("set_pool")
        tanh_r, tanh_ar, sin_half, stack_made, stack_ps, stack_sb = [
            sem(n) for n in ("tanh_r", "tanh_ar", "sin_half", "stack_made", "stack_ps", "stack_sb")]
        r_ready, dt_args, half_args = sem("r_ready"), sem("dt_args"), sem("half_args")
        fine_args, fine_sin, fine_exp, fine_pow = sem("fine_args"), sem("fine_sin"), sem("fine_exp"), sem("fine_pow")
        coarse_args, coarse_sin, coarse_exp, coarse_pow = sem("coarse_args"), sem("coarse_sin"), sem("coarse_exp"), sem("coarse_pow")
        k_taps_ps, k_taps_sb, k_out, k_back, kf_ps = sem("k_taps_ps"), sem("k_taps_sb"), sem("k_out"), sem("k_back"), sem("kf_ps")
        ones_made, vec_ps, vec_sb, wv_ps, wv_sb = sem("ones_made"), sem("vec_ps"), sem("vec_sb"), sem("wv_ps"), sem("wv_sb")
        film_w, wvf_ps, tm_made, tm_ps, b1_ps = sem("film_w"), sem("wvf_ps"), sem("tm_made"), sem("tm_ps"), sem("b1_ps")
        row_sums, sums0, sums1, const_ps, gates_tanh = [sem(n) for n in ("row_sums", "sums0", "sums1", "const_ps", "gates_tanh")]

        x_in = sem("x_in")
        ctx_in, vmask_in, out_sent = sem("ctx_in"), sem("vmask_in"), sem("out_sent")
        dve_own, pool_own = sem("dve_own"), sem("pool_own")
        ln_stats, ln_scales, x0_ready, x0t_ps, ct_ps, x0t_sb, ct_sb, q_ps, q_sb, k_ps, k_sb = [sem(n) for n in (
            "ln_stats", "ln_scales", "x0_ready", "x0t_ps", "ct_ps", "x0t_sb", "ct_sb", "q_ps", "q_sb", "k_ps", "k_sb")]
        vwf_ps, vwf_sb, sc_ps, sc_sb, guard_ready, diff_ready, exp_ready, recip_ready, prob_ready, attn_ready = [sem(n) for n in (
            "vwf_ps", "vwf_sb", "sc_ps", "sc_sb", "guard_ready", "diff_ready", "exp_ready", "recip_ready", "prob_ready", "attn_ready")]
        at_ps, at_sb, film_ps, film_sb, xm_ready, xd_ready, spec_ps, spec_mul, spec_ready = [sem(n) for n in (
            "at_ps", "at_sb", "film_ps", "film_sb", "xm_ready", "xd_ready", "spec_ps", "spec_mul", "spec_ready")]
        y_ps, y_mod, xt_ready, hh_ready, ht_ps, ht_sb, xh_ps, gx_done, xo_ps, xo_add, xt2_ready = [sem(n) for n in (
            "y_ps", "y_mod", "xt_ready", "hh_ready", "ht_ps", "ht_sb", "xh_ps", "gx_done", "xo_ps", "xo_add", "xt2_ready")]
        n_ready, xnew_ready, xf_ready, xft_ps, xt_turned = [sem(n) for n in (
            "n_ready", "xnew_ready", "xf_ready", "xft_ps", "xt_turned")]
        res_ready, gl_ps, gl_sb, gdiff, gexp, wp_ready, wt_ps, wt_sb, wb_ps, wb_sb = [sem(n) for n in (
            "res_ready", "gl_ps", "gl_sb", "gdiff", "gexp", "wp_ready", "wt_ps", "wt_sb", "wb_ps", "wb_sb")]
        tanh_done, basis_ready, basis_used, l0_ps, zc_ready, zq_ready, var_ps, var_sb, rstd_ready, dg_ready, rb_ps, h1_ready = [
            sem(n) for n in ("tanh_done", "basis_ready", "basis_used", "l0_ps", "zc_ready", "zq_ready", "var_ps", "var_sb",
                             "rstd_ready", "dg_ready", "rb_ps", "h1_ready")]
        mh_ps, mg_done, mg_used, o_ps, part_ready, acc_ready, yt_ps, y_ready = [sem(n) for n in (
            "mh_ps", "mg_done", "mg_used", "o_ps", "part_ready", "acc_ready", "yt_ps", "y_ready")]
        arrive = sem("arrive")
        round_sems = range(x_in.num, arrive.num + 1)
        go = {n: sem("go_" + n) for n in ("tensor", "scalar", "vector", "gpsimd")}

        block = ctx.enter_context(nc.Block())

        STEPS = {"attention": attention_steps(), "mixture": mixture_steps(), "both": both_steps()}

        def meet(eng, name):
            if name == "sync":
                eng.wait_ge(arrive, 4)
                eng.sem_clear(round_sems)
                for s in go.values():
                    eng.sem_inc(s, 1)
            else:
                eng.drain().then_inc(arrive, 1)
                eng.wait_ge(go[name], 1)
                eng.sem_clear(go[name])

        def rounds(eng, name, steps, counts):
            def one(kind, mixed, attended):
                counts.clear()
                counts.update(made=0, used=0, hidden=0, wb=0, out=0, own=0, h1=0, turned=0, var=0)
                for s in STEPS[kind]:
                    if s[0] in steps:
                        steps[s[0]](mixed, attended, *s[1:])
                if kind != "attention" and "end" in steps:
                    steps["end"](mixed, attended)
                meet(eng, name)

            meet(eng, name)
            one("attention", None, 0)
            with eng.Fori(0, NGROUPS - 1) as i:
                one("both", i, i + 1)
            one("mixture", NGROUPS - 1, None)

        @block.sync
        def _(sp):
            for dst, src in ((misc[:, :], a["c_misc"]), (ident[:, :], a["c_ident"]), (dft[:, :, :], a["c_dft"]),
                             (esel_in, a["c_esel"])):
                sp.dma_start(dst, src).then_inc(in_const, 16)
            sp.dma_start(wvin[0:DV, :], a["L0_xattn_Wv"]).then_inc(in_film, 16)
            sp.dma_start(wfilm[:, 0:2 * D], a["L0_xattn_W_film_in"]).then_inc(in_film, 16)
            sp.dma_start(wfilm[:, 2 * D:4 * D], a["L0_xattn_W_film_out"]).then_inc(in_film, 16)
            sp.dma_start(brow[:, 0:2 * D], a["L0_xattn_b_film_in"].rearrange("(a n) -> a n", a=1)).then_inc(in_film, 16)
            sp.dma_start(brow[:, 2 * D:4 * D], a["L0_xattn_b_film_out"].rearrange("(a n) -> a n", a=1)).then_inc(in_film, 16)
            sp.dma_start(gnin, a["L0_xattn_g_norm_in"].partition_broadcast(P)).then_inc(in_film, 16)
            sp.dma_start(bnin, a["L0_xattn_b_norm_in"].partition_broadcast(P)).then_inc(in_film, 16)
            sp.dma_start(gates[:, 0:1], a["L0_xattn_mod_gate"].partition_broadcast(P)).then_inc(in_film, 16)
            sp.dma_start(gates[:, 1:2], a["g_xattn"].partition_broadcast(P)).then_inc(in_film, 16)
            sp.dma_start(gates[:, 2:3], a["g_ffn"].partition_broadcast(P)).then_inc(in_film, 16)
            for n, k in VECS:
                src = a[n].rearrange("e (h p) -> (e h) p", p=P) if len(a[n].shape) == 2 else a[n].rearrange("(h p) -> h p", p=P)
                sp.dma_start(vrows[ROW_OF[n]:ROW_OF[n] + k, :], src).then_inc(in_vec, 16)
            sp.dma_start(xw1[:, :], a["L0_xattn_W1"]).then_inc(in_xmlp, 16)
            sp.dma_start(xw2[:, :, :], a["L0_xattn_W2"].rearrange("(c p) d -> p c d", p=P)).then_inc(in_xmlp, 16)
            sp.dma_start(gout[:, :], a["L0_xattn_g_norm_out"].partition_broadcast(P)).then_inc(in_xmlp, 16)
            sp.dma_start(bout[:, :], a["L0_xattn_b_norm_out"].partition_broadcast(P)).then_inc(in_xmlp, 16)
            sp.dma_start(b2row[:, :], a["L0_xattn_b2"].partition_broadcast(P)).then_inc(in_xmlp, 16)
            sp.dma_start(wq[:, :], a["L0_xattn_Wq"]).then_inc(in_attn, 16)
            sp.dma_start(wk[0:DV, :], a["L0_xattn_Wk"]).then_inc(in_attn, 16)
            sp.dma_start(tm_u8, a["mask_text"]).then_inc(in_attn, 16)
            sp.dma_start(tiny[:, 0:1], a["L0_xattn_log_dt"].rearrange("(p a) -> p a", a=1)).then_inc(in_s4, 16)
            for k, n in enumerate(("A_re", "A_im", "C_re", "C_im")):
                sp.dma_start(s4in[:, k, :], a["L0_xattn_" + n]).then_inc(in_s4, 16)
            sp.dma_start(drow, a["L0_xattn_D_skip"].rearrange("(a p) -> a p", a=1)).then_inc(in_s4, 16)

            def late_loads(mixed, g):
                for e in range(NE):
                    sp.dma_start(kw0[:, e, :, :], a["L0_ffn_kan_sl_W0"][e].rearrange("(p g) o -> p g o", g=NG)).then_inc(in_kw0[e], 16)
                for e in range(NE):
                    for h in range(2):
                        sp.dma_start(kw1[:, e, h * NG:(h + 1) * NG, :],
                                     a["L0_ffn_kan_sl_W1"][e].rearrange("(h p g) o -> h p g o", h=2, g=NG)[h]).then_inc(in_kw1, 16)
                sp.dma_start(gatew[:, :], a["L0_ffn_gate_W"]).then_inc(in_moe, 16)
                for e in range(NE):
                    sp.dma_start(mw1[:, e, :], a["L0_ffn_mlp_W1"][e]).then_inc(in_moe, 16)
                    sp.dma_start(mw2[:, e, :, :], a["L0_ffn_mlp_W2"][e].rearrange("(c p) o -> p c o", p=P)).then_inc(in_moe, 16)

            def s4_taps(mixed, g):
                sp.wait_ge(k_taps_sb, 4)
                sp.dma_start(kscratch.rearrange("(a b) d -> a b d", a=NA), ka).then_inc(k_out, 16)
                sp.wait_ge(k_out, 16)
                sp.dma_start(kl, kscratch).then_inc(k_back, 16)

            def late_loads_in(mixed, g):
                sp.wait_ge(in_moe, 16 * (1 + 2 * NE))

            def load(mixed, g):
                sp.dma_start(xg[:, :, :], a["x"].rearrange("(n b) s d -> n s b d", b=G)[g]).then_inc(x_in, 16)
                sp.dma_start(cg[:, :, :], a["ctx_768"].rearrange("(n b) s d -> n s b d", b=G)[g]).then_inc(ctx_in, 16)
                sp.dma_start(vmu[:, :], a["mask_vision"].rearrange("(n b) k -> n (b k)", b=G)[g].partition_broadcast(P))\
                  .then_inc(vmask_in, 16)

            def finish(g, attended):
                sp.wait_ge(y_ready, 1)
                sp.dma_start(out.rearrange("(n b) s d -> n s b d", b=G)[g], yout).then_inc(out_sent, 16)

            def end(g, attended):
                sp.wait_ge(out_sent, 16)

            rounds(sp, "sync", {"load": load, "finish": finish, "end": end, "late_loads": late_loads, "s4_taps": s4_taps,
                                "late_loads_in": late_loads_in}, {})

        @block.tensor
        def _(pe):
            n = {}

            pe.wait_ge(in_const, 64)
            pe.wait_ge(in_vec, 16 * len(VECS))
            pe.transpose(XA[:, 0:NROWS], vrows[0:NROWS, :], ident[0:NROWS, 0:NROWS]).then_inc(vec_ps, 1)
            pe.wait_ge(in_film, 160)
            pe.transpose(XB[:, 0:DV], wvin[0:DV, :], ident[0:DV, 0:DV]).then_inc(wv_ps, 1)
            pe.wait_ge(tm_made, 1)
            pe.transpose(HA[:, 0:NROW], tm_rows, ident[0:NROW, 0:NROW]).then_inc(tm_ps, 1)
            pe.wait_ge(in_xmlp, 80)
            pe.wait_ge(vec_sb, 1)
            bf = cols[:, ROW_OF["L0_xattn_b_ffn"]:ROW_OF["L0_xattn_b_ffn"] + 1]
            for c in range(HC):
                t = pe.matmul(V[:, c:c + 1], xw1[:, c * P:(c + 1) * P], bf, start=True, stop=True)
            t.then_inc(b1_ps, 1)
            pe.wait_ge(film_w, 3)
            pe.wait_ge(wv_sb, 1)
            pe.matmul(O[0:DV + 1, :], wvt[:, 0:DV + 1], wfs, start=True, stop=False)
            pe.matmul(O[0:DV + 1, :], onehot, brow2, start=False, stop=True).then_inc(wvf_ps, 1)

            def s4_turn(m, g):
                pe.wait_ge(stack_made, 4)
                for k in range(4):
                    t = pe.transpose(Z[0][:, k * P:(k + 1) * P], stack_d[:, k, :], ident[:, :])
                t.then_inc(stack_ps, 1)

            def s4_taps(m, g):
                pe.wait_ge(fine_pow, 1)
                pe.wait_ge(coarse_pow, 1)
                for q, bk in enumerate((Z[0], Z[1], HA, V)):
                    for d in range(32):
                        t = pe.matmul(bk[0:NA, d * NB:(d + 1) * NB], pw_a[:, :, 32 * q + d], pw_r[:, :, 32 * q + d],
                                      start=True, stop=True)
                    t.then_inc(k_taps_ps, 1)

            def s4_spectrum(m, g):
                pe.wait_ge(k_back, 16)
                pe.wait_ge(ones_made, 3)
                pe.matmul(O[:, 0:D], dft[:, 0, :], kl, start=True, stop=False)
                pe.matmul(O[:, 0:D], ones[0:1, :], drow, start=False, stop=True)
                pe.matmul(O[:, D:2 * D], dft[:, 1, :], kl, start=True, stop=True).then_inc(kf_ps, 1)

            def kan_const(m, g):
                pe.wait_ge(k_taps_sb, 4)
                pe.wait_ge(sums0, NE)
                pe.wait_ge(sums1, NE)
                for e in range(NE):
                    for h in range(2):
                        pe.matmul(V[:, 2 * e + h:2 * e + h + 1], sum0[:, e, h * P:(h + 1) * P], ones[:, 0:1],
                                  start=True, stop=True)
                    pe.matmul(V[:, 2 * NE + e:2 * NE + e + 1], sum1[:, e, :], ones[:, 0:1], start=True, stop=True)
                sb0 = cols[:, ROW_OF["L0_ffn_kan_sl_b0"]:ROW_OF["L0_ffn_kan_sl_b0"] + 2 * NE].rearrange("p (e h) -> p h e", h=2)
                for h in range(2):
                    t = pe.matmul(V[:, 3 * NE:4 * NE], mean_w[:, :], sb0[:, h, :], start=(h == 0), stop=(h == 1))
                t.then_inc(const_ps, 1)

            def qk_turn(m, g):
                pe.wait_ge(x0_ready, 1)
                for b in range(G):
                    t = pe.transpose(XA[:, b * S:(b + 1) * S], x0[:, b, :], ident[:, :])
                t.then_inc(x0t_ps, 1)
                pe.wait_ge(ctx_in, 16)
                for b in range(G):
                    t = pe.transpose(XB[0:DV, b * NK:(b + 1) * NK], cg[:, b, :], ident[0:NK, 0:NK])
                t.then_inc(ct_ps, 1)

            def qk(m, g):
                pe.wait_ge(x0t_sb, 1)
                pe.matmul(XA[:, :], wq[:, :], x0t[:, :], start=True, stop=True).then_inc(q_ps, 1)
                pe.wait_ge(ct_sb, 1)
                pe.matmul(XB[:, 0:G * NK].rearrange("p (b k) -> p b k", b=G), wk[0:DV, :], ct[0:DV, :, 0:NK],
                          start=True, stop=True).then_inc(k_ps, 1)

            def vwf_(m, g):
                for b, bk in enumerate((XC, XA, XB, XC)):
                    if b == 1:
                        pe.wait_ge(q_sb, 1)
                    if b == 2:
                        pe.wait_ge(k_sb, 1)
                    if b == 3:
                        pe.wait_ge(vwf_sb, 1)
                    pe.matmul(bk[0:NK + 1, :], ct[0:DV + 1, b, :], wvf[0:DV + 1, :], start=True, stop=True).then_inc(vwf_ps, 1)

            def scores(m, g, b0):
                for b in (b0, b0 + 1):
                    if b == 0:
                        pe.wait_ge(vwf_sb, 2)
                    if b == 1:
                        pe.wait_ge(vwf_sb, 3)
                    if b >= 2:
                        pe.wait_ge(sc_sb, b - 1)
                    pe.matmul((XA, XB)[b % 2][:, 0:H * NK], qt[:, b * S:(b + 1) * S],
                              kblk[:, b, :, :].rearrange("p h k -> p (h k)"), start=True, stop=True).then_inc(sc_ps, 1)

            def attn_turn(m, g):
                pe.wait_ge(attn_ready, 1)
                for b in range(G):
                    t = pe.transpose(XA[0:NK + 1, b * S:(b + 1) * S], attn[:, b, :], ident[:, :])
                t.then_inc(at_ps, 1)

            def film_(m, g):
                pe.wait_ge(at_sb, 1)
                pe.wait_ge(vwf_sb, 4)
                for b in range(G):
                    if b >= 2:
                        pe.wait_ge(film_sb, b - 1)
                    pe.matmul((XB, XC)[b % 2][:, :], attnt[0:NK + 1, b * S:(b + 1) * S], vwf[0:NK + 1, b, :],
                              start=True, stop=True).then_inc(film_ps, 1)

            def conv_a(m, g):
                pe.wait_ge(xm_ready, 1)
                pe.wait_ge(film_sb, 4)
                for k, bk in enumerate((XA, XB)):
                    pe.matmul(bk[:, :], dft[:, k, :], qt[:, :], start=True, stop=True).then_inc(spec_ps, 1)

            def conv_c(m, g):
                pe.wait_ge(spec_ready, 2)
                pe.matmul(XC[:, :], dft[:, 2, :], spec[:, 0, :], start=True, stop=False)
                pe.matmul(XC[:, :], dft[:, 3, :], spec[:, 2, :], start=False, stop=True).then_inc(y_ps, 1)

            def ht_turn(m, g):
                pe.wait_ge(hh_ready, 1)
                for b in range(G):
                    t = pe.transpose(XA[:, b * S:(b + 1) * S], hh[:, b, :], ident[:, :])
                t.then_inc(ht_ps, 1)

            def xmlp_a(m, g):
                pe.wait_ge(ht_sb, 1)
                for c in range(HC):
                    if c == 3:
                        pe.wait_ge(gx_done, 1)
                    pe.matmul((XB, XC, XA, XB)[c][:, :], xw1[:, c * P:(c + 1) * P], ht[:, :], start=True, stop=True)\
                      .then_inc(xh_ps, 1)

            def xmlp_b(m, g):
                pe.wait_ge(gx_done, HC)
                for b in range(G):
                    for c in range(HC):
                        t = pe.matmul(XC[:, b * D:(b + 1) * D], gx[:, c, b * S:(b + 1) * S], xw2[:, c, :],
                                      start=(c == 0), stop=(c == HC - 1))
                t.then_inc(xo_ps, 1)

            def xt_turn(m, g):
                for k, (bk, src) in enumerate(((XA, hh), (XB, xh))):
                    pe.wait_ge(xf_ready, k + 1)
                    for b in range(G):
                        t = pe.transpose(bk[:, b * S:(b + 1) * S], src[:, b, :], ident[:, :])
                    t.then_inc(xft_ps, 1)

            def v_free():
                pe.wait_ge(gl_sb, 1)
                if n["hidden"]:
                    pe.wait_ge(mg_done, n["hidden"])
                if n["var"]:
                    pe.wait_ge(var_sb, n["var"])
                if n["h1"]:
                    pe.wait_ge(h1_ready, 2 * n["h1"])

            def ha_free():
                if n["turned"]:
                    pe.wait_ge(wt_sb, 1)
                if n["hidden"]:
                    pe.wait_ge(mg_done, n["hidden"])
                if n["wb"]:
                    pe.wait_ge(wb_sb, n["wb"])

            def gate_a(g, m):
                for b in range(G):
                    t = pe.matmul(V[:, b * NX:(b + 1) * NX], xft[:, b * S:(b + 1) * S], gatew[:, :], start=True, stop=True)
                t.then_inc(gl_ps, 1)

            def gate_d(g, m):
                pe.wait_ge(wp_ready, 1)
                ha_free()
                n["turned"] = 1
                hb = HA[0:3 * NX, 0:GT // 2].bitcast(BF16)
                for b in range(G):
                    t = pe.transpose(hb[:, b * S:(b + 1) * S], wp[:, b, :, :].rearrange("p k e -> p (k e)"), identb[:, :])
                t.then_inc(wt_ps, 1)

            def wb(g, m, i):
                pe.wait_ge(wt_sb, 1)
                ha_free()
                pe.matmul(HA[:, :], esel[:, OUTS[i], :], wt[:, :], start=True, stop=True).then_inc(wb_ps, 1)
                n["wb"] += 1

            def use(g, m):
                for c in range(n["used"], n["used"] + STEP):
                    e, layer, k = CHUNKS[c]
                    if k == 0 and layer == 0 and e > 0:
                        pe.wait_ge(zc_ready, 2 * e)
                    if k == 0 and layer == 1 and n["out"]:
                        pe.wait_ge(part_ready, n["out"])
                    pe.wait_ge(basis_ready, c + 1)
                    if layer == 0:
                        for h in range(2):
                            t = pe.matmul(Z[h][:, :], kw0[:, e, k, h * P:(h + 1) * P], ring[:, c % RING, :],
                                          start=(k == 0), stop=(k == NG - 1))
                    else:
                        t = pe.matmul(O[:, :], kw1[:, e, k, :], ring[:, c % RING, :], start=(k == 0), stop=(k == 2 * NG - 1))
                        if k == 2 * NG - 1:
                            n["out"] += 1
                    t.then_inc(basis_used, 1)
                n["used"] += STEP

            def hidden(e, c):
                if c % 2 == 0:
                    ha_free()
                else:
                    v_free()
                pe.matmul((HA, V)[c % 2][:, :], mw1[:, e, c * P:(c + 1) * P], xft[:, :], start=True, stop=True)\
                  .then_inc(mh_ps, 1)

            def output(e, c):
                if c == 0 and n["out"]:
                    pe.wait_ge(part_ready, n["out"])
                pe.wait_ge(mg_done, HC * e + c + 1)
                pe.matmul(O[:, :], mw2[:, e, c, :], mg[:, c % 2, :], start=(c == 0), stop=(c == HC - 1)).then_inc(mg_used, 1)

            def mlp_a(g, m, e):
                hidden(e, 0)
                hidden(e, 1)
                n["hidden"] += 2

            def mlp_b(g, m, e):
                output(e, 0)
                output(e, 1)
                hidden(e, 2)
                hidden(e, 3)
                n["hidden"] += 2

            def mlp_c(g, m, e):
                output(e, 2)
                output(e, 3)
                n["out"] += 1

            def var_a(g, m, e):
                pe.wait_ge(zq_ready, 2 * e + 2)
                v_free()
                for b in range(G):
                    for h in range(2):
                        t = pe.matmul(V[:, b:b + 1], zq[:, h, b * S:(b + 1) * S], mean_w[:, 0:1], start=(h == 0), stop=(h == 1))
                t.then_inc(var_ps, 1)
                n["var"] += 1

            def var_b(g, m, e):
                pe.wait_ge(dg_ready, e + 1)
                v_free()
                pe.matmul(V[:, :], ones[:, :], dg[:, :, :].rearrange("p b t -> p (b t)"), start=True, stop=True).then_inc(rb_ps, 1)
                n["h1"] += 1

            def finish(g, m):
                pe.wait_ge(acc_ready, NX)
                for b in range(G):
                    t = pe.transpose(O[:, b * D:(b + 1) * D], acc[:, b * S:(b + 1) * S], ident[:, :])
                t.then_inc(yt_ps, 1)

            steps = dict(s4_turn=s4_turn, s4_taps=s4_taps, s4_spectrum=s4_spectrum, kan_const=kan_const,
                         qk_turn=qk_turn, qk=qk, vwf=vwf_, scores=scores, attn_turn=attn_turn, film=film_, conv_a=conv_a,
                         conv_c=conv_c, ht_turn=ht_turn, xmlp_a=xmlp_a, xmlp_b=xmlp_b, xt_turn=xt_turn, gate_a=gate_a,
                         gate_d=gate_d, wb=wb, use=use, mlp_a=mlp_a, mlp_b=mlp_b, mlp_c=mlp_c, var_a=var_a, var_b=var_b, finish=finish)
            rounds(pe, "tensor", steps, n)

        @block.scalar
        def _(act):
            n = {}

            def copy(dst, src):
                return act.activation(dst, src, ACT.Copy)

            act.wait_ge(in_film, 160)
            act.activation(gtanh[:, :], gates[:, 1:3], ACT.Tanh).then_inc(gates_tanh, 1)
            act.wait_ge(vec_ps, 1)
            copy(cols[:, :], XA[:, 0:NROWS]).then_inc(vec_sb, 1)
            act.wait_ge(wv_ps, 1)
            copy(wvt[:, 0:DV], XB[:, 0:DV]).then_inc(wv_sb, 1)
            act.wait_ge(tm_ps, 1)
            copy(tmt[:, :], HA[:, 0:NROW]).then_inc(wv_sb, 1)
            act.wait_ge(wvf_ps, 1)
            copy(wvf[0:DV + 1, :], O[0:DV + 1, :])

            def s4_dt(m, g):
                act.wait_ge(r_ready, 1)
                act.activation(tiny[:, 4:5], tiny[:, 3:4], ACT.Tanh, scale=0.5).then_inc(tanh_r, 1)

            def s4_half(m, g):
                act.wait_ge(dt_args, 1)
                act.activation(s4t[:, 3, :], s4t[:, 0, :], ACT.Tanh, scale=0.5).then_inc(tanh_ar, 1)
                act.wait_ge(half_args, 2)
                act.activation(s4t[:, 5, :], s4t[:, 4, :], ACT.Sin, scale=TWO_PI).then_inc(sin_half, 1)
                act.activation(s4t[:, 7, :], s4t[:, 6, :], ACT.Sin, scale=TWO_PI).then_inc(sin_half, 1)

            def s4_turn(m, g):
                act.wait_ge(stack_ps, 1)
                copy(acc[:, :], Z[0][:, :]).then_inc(stack_sb, 1)

            def s4_exp(m, g):
                act.wait_ge(stack_sb, 1)
                for b in range(NB):
                    t = act.activation(pw_e[:, b, :], stk[:, 0, :], ACT.Exp, scale=float(b))
                t.then_inc(fine_exp, 1)
                for i in range(NA):
                    t = act.activation(pw_a[:, i, :], stk[:, 0, :], ACT.Exp, scale=float(NB * i))
                t.then_inc(coarse_exp, 1)

            def s4_args(m, g):
                act.wait_ge(fine_args, 1)
                act.activation(pw_r, pw_r, ACT.Sin, scale=TWO_PI).then_inc(fine_sin, 1)
                act.wait_ge(coarse_args, 1)
                act.activation(pw_cs, pw_cs, ACT.Sin, scale=TWO_PI).then_inc(coarse_sin, 1)

            def s4_taps(m, g):
                act.wait_ge(fine_pow, 1)
                act.wait_ge(coarse_pow, 1)
                for q, bk in enumerate((Z[0], Z[1], HA, V)):
                    act.wait_ge(k_taps_ps, q + 1)
                    copy(ka[:, :, 32 * q:32 * q + 32], bk[0:NA, :].rearrange("p (d b) -> p b d", b=NB)).then_inc(k_taps_sb, 1)

            def s4_spectrum(m, g):
                act.wait_ge(kf_ps, 1)
                copy(kf[:, :, :].rearrange("p k d -> p (k d)"), O[:, 0:2 * D])

            def qk_turn(m, g):
                act.wait_ge(x0t_ps, 1)
                copy(x0t[:, :], XA[:, :]).then_inc(x0t_sb, 1)
                act.wait_ge(ct_ps, 1)
                copy(ct[0:DV, :, 0:NK], XB[0:DV, 0:G * NK].rearrange("p (b k) -> p b k", b=G)).then_inc(ct_sb, 1)

            def qk(m, g):
                act.wait_ge(q_ps, 1)
                copy(qt[:, :], XA[:, :]).then_inc(q_sb, 1)

            def vwf_(m, g):
                for b, bk in enumerate((XC, XA, XB, XC)):
                    act.wait_ge(vwf_ps, b + 1)
                    copy(vwf[0:NK + 1, b, :], bk[0:NK + 1, :]).then_inc(vwf_sb, 1)

            def probs_b(m, g):
                act.wait_ge(diff_ready, 1)
                act.activation(scr[:, :, :, :], scr[:, :, :, :], ACT.Exp, scale=SCALE).then_inc(exp_ready, 1)

            def attn_turn(m, g):
                act.wait_ge(at_ps, 1)
                copy(attnt[0:NK + 1, :], XA[0:NK + 1, :]).then_inc(at_sb, 1)

            def film_(m, g):
                for b in range(G):
                    act.wait_ge(film_ps, b + 1)
                    copy(film[:, b, :], (XB, XC)[b % 2][:, :]).then_inc(film_sb, 1)

            def ht_turn(m, g):
                act.wait_ge(ht_ps, 1)
                copy(ht[:, :], XA[:, :]).then_inc(ht_sb, 1)

            def xmlp_a(m, g):
                for c in range(HC):
                    act.wait_ge(xh_ps, c + 1)
                    act.activation(gx[:, c, :], (XB, XC, XA, XB)[c][:, :], ACT.Gelu, bias=xb1[:, c:c + 1]).then_inc(gx_done, 1)

            def xt_turn(m, g):
                if m is not None:
                    act.wait_ge(tanh_done, CHUNKS.index((NE - 1, 0, NG - 1)) + 1)
                for k, (dst, bk) in enumerate(((xft, XA), (xkt, XB))):
                    act.wait_ge(xft_ps, k + 1)
                    copy(dst[:, :], bk[:, :]).then_inc(xt_turned, 1)

            def gate_b(g, m):
                act.wait_ge(gdiff, 1)
                act.activation(gs[:, 1, :], gs[:, 0, :], ACT.Exp).then_inc(gexp, 1)

            def wb(g, m, i):
                act.wait_ge(wb_ps, i + 1)
                if i >= 3:
                    act.wait_ge(part_ready, i - 2)
                copy(wbs[:, i % 3, :], HA[:, :]).then_inc(wb_sb, 1)

            def tanh(g, m):
                for c in range(n["made"], n["made"] + STEP):
                    e, layer, k = CHUNKS[c]
                    if c >= RING:
                        act.wait_ge(basis_used, c - RING + 1)
                    if layer == 0:
                        src, sc, bi = xkt[:, :], scale0[:, e:e + 1], bias0[:, e, k:k + 1]
                    else:
                        h = k // NG
                        if k == 0:
                            act.wait_ge(h1_ready, 2 * e + 2)
                        src, sc, bi = h1[:, e % 2, h, :], scale1[:, 2 * e + h:2 * e + h + 1], bias1[:, 2 * e + h, k % NG:k % NG + 1]
                    act.activation(ring[:, c % RING, :], src, ACT.Tanh, bias=bi, scale=sc).then_inc(tanh_done, 1)
                n["made"] += STEP

            def gelu(e, c):
                b1 = ROW_OF["L0_ffn_mlp_b1"] + HC * e + c
                act.wait_ge(mh_ps, HC * e + c + 1)
                if HC * e + c >= 2:
                    act.wait_ge(mg_used, HC * e + c - 1)
                act.activation(mg[:, c % 2, :], (HA, V)[c % 2][:, :], ACT.Gelu, bias=cols[:, b1:b1 + 1]).then_inc(mg_done, 1)

            def mlp_a(g, m, e):
                gelu(e, 0)
                gelu(e, 1)

            def mlp_b(g, m, e):
                gelu(e, 2)
                gelu(e, 3)

            steps = dict(s4_dt=s4_dt, s4_half=s4_half, s4_turn=s4_turn, s4_exp=s4_exp, s4_args=s4_args, s4_taps=s4_taps,
                         s4_spectrum=s4_spectrum, qk_turn=qk_turn, qk=qk, vwf=vwf_, probs_b=probs_b, attn_turn=attn_turn, film=film_, ht_turn=ht_turn,
                         xmlp_a=xmlp_a, xt_turn=xt_turn, gate_b=gate_b, wb=wb, tanh=tanh, mlp_a=mlp_a, mlp_b=mlp_b)
            rounds(act, "scalar", steps, n)

        @block.gpsimd
        def _(pool):
            n = {}

            pool.memset(ones[:, :], 1.0).then_inc(ones_made, 1)
            pool.memset(mean_w[:, :], 1.0 / F2).then_inc(ones_made, 1)
            pool.memset(minus_half[:, :], -0.5).then_inc(ones_made, 1)
            pool.memset(kblk[:, :, :, :], 0.0)
            pool.memset(attn[:, :, :], 1.0)
            pool.memset(ct[:, :, :], 0.0).then_inc(set_pool, 1)
            pool.wait_ge(set_pool, 1)
            pool.memset(ct[DV:DV + 1, :, NK:NK + 1], 1.0).then_inc(set_pool, 1)
            pool.wait_ge(set_pool, 2)

            def kan0(m, g, e):
                pool.wait_ge(row_sums, e + 1)
                pool.tensor_tensor(kw0[:, e, :, :], kw0[:, e, :, :], rsum[:, e, :].unsqueeze(2).broadcast_to([P, NG, F2]),
                                   ALU.subtract)

            def link(ins):
                n["own"] += 1
                ins.then_inc(pool_own, 1)
                pool.wait_ge(pool_own, n["own"])

            def ln_scale(q, twice):
                pool.wait_ge(ln_stats, q + 1)
                t, r, v, rr = (sml[:, 4 * q + k, :] for k in range(4))
                var = mv[:, :, 1]
                link(pool.tensor_scalar(t, var, EPS, None, ALU.add))
                ins = pool.tensor_tensor(r, t, minus_half[:, :], ALU.pow)
                if twice:
                    link(ins)
                    link(pool.tensor_tensor(v, var, r, ALU.mult))
                    link(pool.tensor_tensor(v, v, r, ALU.mult))
                    link(pool.tensor_scalar(v, v, EPS, None, ALU.add))
                    link(pool.tensor_tensor(t, v, minus_half[:, :], ALU.pow))
                    ins = pool.tensor_tensor(rr, r, t, ALU.mult)
                ins.then_inc(ln_scales, 1)

            def probs_a(m, g):
                pool.wait_ge(guard_ready, 1)
                s3 = scr[:, :, :, :].rearrange("p b h k -> p (b h) k")
                pool.tensor_tensor(s3, s3, sm16[:, 0, :].unsqueeze(2).broadcast_to([P, G * H, NK]), ALU.subtract)\
                    .then_inc(diff_ready, 1)

            def probs_c(m, g):
                pool.wait_ge(recip_ready, 1)
                s3 = scr[:, :, :, :].rearrange("p b h k -> p (b h) k")
                pool.tensor_tensor(s3, s3, sm16[:, 3, :].unsqueeze(2).broadcast_to([P, G * H, NK]), ALU.mult)\
                    .then_inc(prob_ready, 1)

            def modulate(m, g):
                pool.wait_ge(film_sb, 4)
                pool.tensor_tensor(x0[:, :, :], x0[:, :, :], film[:, :, 3 * D:4 * D], ALU.add).then_inc(xd_ready, 1)

            def conv_b(m, g):
                pool.wait_ge(spec_mul, 2)
                pool.tensor_tensor(spec[:, 0, :], spec[:, 0, :], spec[:, 1, :], ALU.subtract).then_inc(spec_ready, 1)
                pool.wait_ge(spec_mul, 4)
                pool.tensor_tensor(spec[:, 2, :], spec[:, 2, :], spec[:, 3, :], ALU.add).then_inc(spec_ready, 1)

            def conv_d(m, g):
                pool.wait_ge(y_mod, 1)
                pool.wait_ge(xd_ready, 1)
                pool.tensor_tensor(xt[:, :, :], xm, xt[:, :, :], ALU.add).then_inc(xt_ready, 1)

            def xmlp_b(m, g):
                pool.wait_ge(xo_add, 1)
                pool.tensor_tensor(xt[:, :, :], xt[:, :, :], b2row[:, :].unsqueeze(1).broadcast_to([P, G, D]), ALU.add)\
                    .then_inc(xt2_ready, 1)

            def ln3_out(m, g):
                pool.wait_ge(n_ready, 1)
                if m is not None:
                    pool.wait_ge(res_ready, 1)
                link(pool.tensor_tensor(xnew[:, :, :], hh, gout[:, :].unsqueeze(1).broadcast_to([P, G, D]), ALU.mult))
                link(pool.tensor_tensor(xnew[:, :, :], xnew[:, :, :], bout[:, :].unsqueeze(1).broadcast_to([P, G, D]), ALU.add))
                pool.tensor_tensor(xnew[:, :, :], xnew[:, :, :], xg[:, :, :], ALU.add).then_inc(xnew_ready, 1)

            def start(g, m):
                pool.tensor_copy(xres[:, :, :], xnew[:, :, :]).then_inc(res_ready, 1)

            def z_out(g, m, e):
                for h in range(2):
                    pool.wait_ge(zc_ready, 2 * e + h + 1)
                    pool.tensor_tensor(zq[:, h, :], zc[:, h, :], zc[:, h, :], ALU.mult).then_inc(zq_ready, 1)

            def var_a(g, m, e):
                pool.wait_ge(var_sb, e + 1)
                pool.tensor_tensor(vv[:, 1, :], vv[:, 0, :], minus_half[:, :], ALU.pow).then_inc(rstd_ready, 1)

            def comb(g, m, i):
                pool.wait_ge(part_ready, i + 1)
                if i == 0:
                    pool.tensor_copy(acc[:, :], part[:, 0, :]).then_inc(acc_ready, 1)
                    return
                pool.wait_ge(acc_ready, i)
                pool.tensor_tensor(acc[:, :], acc[:, :], part[:, i % 2, :], ALU.subtract if OUTS[i] >= NE else ALU.add)\
                    .then_inc(acc_ready, 1)

            steps = dict(kan0=kan0, ln1=lambda m, g: ln_scale(0, True), ln2=lambda m, g: ln_scale(1, False),
                         ln3=lambda m, g: ln_scale(2, False), ln4=lambda m, g: ln_scale(3, True),
                         probs_a=probs_a, probs_c=probs_c, modulate=modulate, conv_b=conv_b, conv_d=conv_d,
                         xmlp_b=xmlp_b, ln3_out=ln3_out, start=start, z_out=z_out, var_a=var_a, comb=comb)
            rounds(pool, "gpsimd", steps, n)

        @block.vector
        def _(dve):
            n = {}
            done = [0]
            chain = sem("set_chain")

            def step(ins):
                done[0] += 1
                ins.then_inc(chain, 1)
                dve.wait_ge(chain, done[0])

            ts, tt = dve.tensor_scalar, dve.tensor_tensor

            dve.wait_ge(in_film, 160)
            gate = gates[:, 0:1]
            step(ts(wfilm, wfilm, gate, None, ALU.mult))
            step(ts(brow, brow, gates[0:1, 0:1], None, ALU.mult))
            step(ts(brow[:, 0:D], brow[:, 0:D], 1.0, None, ALU.add))
            step(ts(brow[:, 2 * D:3 * D], brow[:, 2 * D:3 * D], 1.0, None, ALU.add))
            for w, o, k in ((wfilm, wfs, P), (brow, brow2, 1)):
                step(tt(o[:, 0:D], w[:, 0:D], gnin[0:k, :], ALU.mult))
                step(tt(o[:, D:2 * D], w[:, 0:D], bnin[0:k, :], ALU.mult))
                step(tt(o[:, D:2 * D], o[:, D:2 * D], w[:, D:2 * D], ALU.add))
                ts(o[:, 2 * D:4 * D], w[:, 2 * D:4 * D], 1.0, None, ALU.mult).then_inc(film_w, 1)
            step(dve.memset(onehot, 0.0))
            step(dve.memset(wvt[:, DV:DV + 1], 0.0))
            dve.memset(onehot[:, DV:DV + 1], 1.0).then_inc(film_w, 1)
            dve.wait_ge(in_attn, 48)
            dve.tensor_copy(tm_rows, tm_u8).then_inc(tm_made, 1)
            dve.wait_ge(in_const, 64)
            dve.wait_ge(vec_sb, 1)
            dve.tensor_copy(identb[:, :], ident[:, :])
            dve.tensor_copy(esel[:, :, :], esel_in).then_inc(set_dve, 1)
            dve.wait_ge(b1_ps, 1)
            r = ROW_OF["L0_xattn_b1"]
            tt(xb1[:, :], V[:, 0:HC], cols[:, r:r + HC], ALU.add).then_inc(set_dve, 1)
            r = ROW_OF["L0_xattn_g_ffn"]
            ts(xw1[:, :], xw1[:, :], cols[:, r:r + 1], None, ALU.mult).then_inc(set_dve, 1)
            dve.wait_ge(gates_tanh, 1)
            ts(gout[:, :], gout[:, :], gtanh[:, 0:1], None, ALU.mult)
            ts(bout[:, :], bout[:, :], gtanh[:, 0:1], None, ALU.mult)
            grid = misc[:, 9:17]
            for g_, b_, sc_, bi_, k in (("L0_ffn_kan_ln_g0", "L0_ffn_kan_ln_b0", scale0, bias0, NE),
                                        ("L0_ffn_kan_ln_g1", "L0_ffn_kan_ln_b1", scale1, bias1, 2 * NE)):
                ts(sc_[:, :], cols[:, ROW_OF[g_]:ROW_OF[g_] + k], 0.5, None, ALU.mult)
                step(ts(cols[:, ROW_OF[b_]:ROW_OF[b_] + k], cols[:, ROW_OF[b_]:ROW_OF[b_] + k], 0.5, None, ALU.mult))
                tt(bi_[:, :, :], cols[:, ROW_OF[b_]:ROW_OF[b_] + k].unsqueeze(2).broadcast_to([P, k, NG]),
                   grid.unsqueeze(1).broadcast_to([P, k, NG]), ALU.add)

            c = [tiny[:, k:k + 1] for k in range(10)]
            dt = c[8]
            q = [s4t[:, k, :] for k in range(20)]
            a_re, a_im, c_re, c_im = (s4in[:, k, :] for k in range(4))

            def s4_dt(m, g):
                dve.wait_ge(in_s4, 96)
                step(ts(c[1], c[0], LOG2E, None, ALU.mult))
                step(ts(c[1], c[1], ROUND, ROUND, ALU.add, ALU.subtract))
                step(ts(c[2], c[1], -LN2_HI, None, ALU.mult))
                step(tt(c[2], c[0], c[2], ALU.add))
                step(ts(c[3], c[1], -LN2_LO, None, ALU.mult))
                step(tt(c[3], c[2], c[3], ALU.add))
                ts(tiny_i[:, :], c[1], 127.0, 8388608.0, ALU.add, ALU.mult).then_inc(r_ready, 1)

            def s4_half(m, g):
                dve.wait_ge(tanh_r, 1)
                step(ts(c[5], c[4], -1.0, 1.0, ALU.mult, ALU.add))
                step(ts(c[6], c[4], 1.0, None, ALU.add))
                step(dve.reciprocal(c[7], c[5]))
                step(tt(c[6], c[6], c[7], ALU.mult))
                step(tt(c[8], c[6], tiny_i[:, :].bitcast(F32), ALU.mult))
                step(ts(q[1], a_im, dt, 1.0 / (4 * np.pi), ALU.mult, ALU.mult))
                ts(q[0], a_re, dt, None, ALU.mult).then_inc(dt_args, 1)
                step(ts(q[2], q[1], ROUND, ROUND, ALU.add, ALU.subtract))
                tt(q[4], q[1], q[2], ALU.subtract).then_inc(half_args, 1)
                step(ts(q[8], q[1], 0.25, None, ALU.add))
                step(ts(q[9], q[8], ROUND, ROUND, ALU.add, ALU.subtract))
                tt(q[6], q[8], q[9], ALU.subtract).then_inc(half_args, 1)
                step(ts(q[10], q[1], 2.0, None, ALU.mult))
                step(ts(q[11], q[10], ROUND, ROUND, ALU.add, ALU.subtract))
                step(tt(q[10], q[10], q[11], ALU.subtract))
                step(tt(q[12], a_re, a_re, ALU.mult))
                step(tt(q[13], a_im, a_im, ALU.mult))
                step(tt(q[12], q[12], q[13], ALU.add))
                step(dve.reciprocal(q[13], q[12]))
                step(tt(q[14], c_re, a_re, ALU.mult))
                step(tt(q[15], c_im, a_im, ALU.mult))
                step(tt(q[14], q[14], q[15], ALU.add))
                step(tt(q[14], q[14], q[13], ALU.mult))
                step(tt(q[15], c_im, a_re, ALU.mult))
                step(tt(q[16], c_re, a_im, ALU.mult))
                step(tt(q[15], q[15], q[16], ALU.subtract))
                step(tt(q[15], q[15], q[13], ALU.mult))

            def s4_turn(m, g):
                dve.wait_ge(tanh_ar, 1)
                step(ts(q[12], q[3], -1.0, 1.0, ALU.mult, ALU.add))
                step(dve.reciprocal(q[13], q[12]))
                step(tt(q[12], q[3], q[13], ALU.mult))
                step(ts(q[12], q[12], 2.0, None, ALU.mult))
                dve.wait_ge(sin_half, 2)
                step(tt(q[13], q[5], q[5], ALU.mult))
                step(ts(q[13], q[13], 2.0, None, ALU.mult))
                step(ts(q[16], q[13], -1.0, 1.0, ALU.mult, ALU.add))
                step(tt(q[16], q[16], q[12], ALU.mult))
                step(tt(q[16], q[16], q[13], ALU.subtract))
                step(tt(q[17], q[5], q[7], ALU.mult))
                step(ts(q[18], q[12], 1.0, 2.0, ALU.add, ALU.mult))
                step(tt(q[17], q[17], q[18], ALU.mult))
                step(tt(q[12], q[16], q[14], ALU.mult))
                step(tt(q[13], q[17], q[15], ALU.mult))
                step(tt(q[12], q[12], q[13], ALU.subtract))
                step(tt(q[13], q[16], q[15], ALU.mult))
                step(tt(q[18], q[17], q[14], ALU.mult))
                step(tt(q[13], q[13], q[18], ALU.add))
                for h in range(2):
                    lo, hi = h * NST, (h + 1) * NST
                    dve.tensor_copy(stack_d[:, 0, lo:hi], q[0])
                    dve.tensor_copy(stack_d[:, 1, lo:hi], q[10])
                    ts(stack_d[:, 2, lo:hi], q[12 + h], 2.0 - 4.0 * h, None, ALU.mult).then_inc(stack_made, 1)
                    ts(stack_d[:, 3, lo:hi], q[13 - h], -2.0, None, ALU.mult).then_inc(stack_made, 1)

            def s4_args(m, g):
                dve.wait_ge(stack_sb, 1)
                for b in range(NB):
                    t = ts(pw_r[:, b, :], stk[:, 1, :], float(b), misc[:, 0:1], ALU.mult, ALU.add)
                step(t)
                rr = rounded.rearrange("p (n d) -> p n d", n=NB)
                step(ts(rr, pw_r, ROUND, ROUND, ALU.add, ALU.subtract))
                tt(pw_r, pw_r, rr, ALU.subtract).then_inc(fine_args, 1)
                dve.wait_ge(fine_args, 1)
                for i in range(NA):
                    ts(pw_cs[:, 0, i, :], stk[:, 1, :], float(NB * i), 0.25, ALU.mult, ALU.add)
                    t = ts(pw_cs[:, 1, i, :], stk[:, 1, :], float(NB * i), None, ALU.mult)
                step(t)
                rc = rounded.rearrange("p (c n d) -> p c n d", c=2, n=NA)
                step(ts(rc, pw_cs, ROUND, ROUND, ALU.add, ALU.subtract))
                tt(pw_cs, pw_cs, rc, ALU.subtract).then_inc(coarse_args, 1)

            def s4_pow(m, g):
                dve.wait_ge(fine_sin, 1)
                dve.wait_ge(fine_exp, 1)
                tt(pw_r, pw_r, pw_e, ALU.mult).then_inc(fine_pow, 1)
                dve.wait_ge(coarse_sin, 1)
                dve.wait_ge(coarse_exp, 1)
                step(tt(pw_cs[:, 0], pw_cs[:, 0], stk[:, 2:3, :].broadcast_to([P, NA, D]), ALU.mult))
                step(tt(pw_cs[:, 1], pw_cs[:, 1], stk[:, 3:4, :].broadcast_to([P, NA, D]), ALU.mult))
                step(tt(pw_cs[:, 0], pw_cs[:, 0], pw_cs[:, 1], ALU.add))
                tt(pw_a, pw_a, pw_cs[:, 0], ALU.mult).then_inc(coarse_pow, 1)

            def kan0(m, g, e):
                dve.wait_ge(in_kw0[e], 16)
                step(dve.tensor_reduce(rsum[:, e, :], kw0[:, e, :, :], AX.X, ALU.add))
                step(dve.tensor_reduce(sum0[:, e, :], kw0[:, e, :, :].rearrange("p g o -> p o g"), AX.X, ALU.add))
                step(ts(rsum[:, e, :], rsum[:, e, :], 1.0 / F2, None, ALU.mult))
                dve.tensor_reduce(rsum_all[:, e:e + 1], rsum[:, e, :], AX.X, ALU.add).then_inc(row_sums, 1)
                dve.wait_ge(row_sums, e + 1)
                ts(sum0[:, e, :], sum0[:, e, :], rsum_all[:, e:e + 1], None, ALU.subtract).then_inc(sums0, 1)

            def kan1(m, g, e):
                dve.wait_ge(in_kw1, 32 * NE)
                dve.tensor_reduce(sum1[:, e, :], kw1[:, e, :, :].rearrange("p k o -> p o k"), AX.X, ALU.add).then_inc(sums1, 1)

            def kan_const(m, g):
                dve.wait_ge(const_ps, 1)
                r = ROW_OF["L0_ffn_kan_sl_b0"]
                step(tt(const0[:, :, :].rearrange("p e h -> p (e h)"), V[:, 0:2 * NE], cols[:, r:r + 2 * NE], ALU.add))
                tt(const0[:, :, :], const0[:, :, :], V[:, 3 * NE:4 * NE].unsqueeze(2).broadcast_to([P, NE, 2]), ALU.subtract)
                r = ROW_OF["L0_ffn_kan_sl_b1"]
                tt(const1[:, :], V[:, 2 * NE:3 * NE], cols[:, r:r + NE], ALU.add)

            def link(ins):
                n["own"] += 1
                ins.then_inc(dve_own, 1)
                dve.wait_ge(dve_own, n["own"])

            def stats(src):
                for b in range(G):
                    t = dve.bn_stats(st[:, b, :], src[:, b, :])
                link(t)
                for b in range(G):
                    t = dve.bn_aggr(mv[:, b, :], st[:, b, :])
                t.then_inc(ln_stats, 1)

            def normalise(dst, src, scale):
                for b in range(G):
                    t = ts(dst[:, b, :], src[:, b, :], mv[:, b, 0:1], sml[:, scale, b:b + 1], ALU.subtract, ALU.mult)
                return t

            def ln1(m, g):
                dve.wait_ge(x_in, 16)
                stats(xg)
                if isinstance(g, int):
                    dve.tensor_copy(tmg[:, :], tmt[:, g * G:(g + 1) * G])
                else:
                    dve.tensor_copy(tmg[:, :], tmt[:, bass.ds(g * G, G)])
                dve.wait_ge(vmask_in, 16)
                ts(vmb[:, :], vmu[:, :], BIG, BIG, ALU.mult, ALU.subtract)

            def ln1_out(m, g):
                dve.wait_ge(ln_scales, 1)
                normalise(x0, xg, 1).then_inc(x0_ready, 1)
                link(normalise(xh, xg, 3))

            def qk(m, g):
                dve.wait_ge(k_ps, 1)
                for h in range(H):
                    lo, hi = h * DH, (h + 1) * DH
                    t = dve.tensor_copy(kblk[lo:hi, :, h, :], XB[lo:hi, 0:G * NK].rearrange("p (b k) -> p b k", b=G))
                t.then_inc(k_sb, 1)

            def scores(m, g, b0):
                for b in (b0, b0 + 1):
                    dve.wait_ge(sc_ps, b + 1)
                    tt(scr[:, b, :, :], (XA, XB)[b % 2][:, 0:H * NK].rearrange("p (h k) -> p h k", h=H),
                       vmb[:, b * NK:(b + 1) * NK].unsqueeze(1).broadcast_to([P, H, NK]), ALU.add).then_inc(sc_sb, 1)

            def topk(m, g, b, r):
                if r == 0:
                    dve.wait_ge(sc_sb, b + 1)
                src = scr if r == 0 else left
                for h in range(H):
                    t = dve.max(top[:, b, h, min(r, 1), :], src[:, b, h, :])
                link(t)
                for h in range(H):
                    t = dve.match_replace(out=left[:, b, h, :], in_to_replace=top[:, b, h, min(r, 1), :],
                                          in_values=src[:, b, h, :], imm_value=TAKEN)
                link(t)

            def probs_a(m, g):
                ts(sm16[:, 0, :].rearrange("p (b h) -> p b h", b=G), top[:, :, :, 0, 0], GUARD, None, ALU.max)\
                    .then_inc(guard_ready, 1)

            def probs_c(m, g):
                dve.wait_ge(exp_ready, 1)
                s2 = scr[:, :, :, :].rearrange("p b h k -> p (b h k)")
                link(dve.scalar_tensor_tensor(out=s2, in0=left[:, :, :, :].rearrange("p b h k -> p (b h k)"), scalar=TAKEN,
                                              in1=s2, op0=ALU.is_equal, op1=ALU.mult))
                link(dve.tensor_reduce(sm16[:, 1, :], scr[:, :, :, :].rearrange("p b h k -> p (b h) k"), AX.X, ALU.add))
                link(dve.reciprocal(sm16[:, 2, :], sm16[:, 1, :]))
                dve.scalar_tensor_tensor(out=sm16[:, 3, :].rearrange("p (b h) -> p b h", b=G),
                                         in0=sm16[:, 2, :].rearrange("p (b h) -> p b h", b=G), scalar=1.0 / H,
                                         in1=tmg[:, :].unsqueeze(2).broadcast_to([P, G, H]), op0=ALU.mult, op1=ALU.mult)\
                   .then_inc(recip_ready, 1)

            def attn_sum(m, g):
                dve.wait_ge(prob_ready, 1)
                dve.tensor_reduce(attn[:, :, 0:NK], scr[:, :, :, :].rearrange("p b h k -> p b k h"), AX.X, ALU.add)\
                   .then_inc(attn_ready, 1)

            def modulate(m, g):
                dve.wait_ge(film_sb, 4)
                link(tt(xm, xh[:, :, :], film[:, :, 0:D], ALU.mult))
                tt(xm, xm, film[:, :, D:2 * D], ALU.add).then_inc(xm_ready, 1)

            def conv_b(m, g):
                for k, (bk, c_) in enumerate(((XA, 0), (XB, 1), (XA, 1), (XB, 0))):
                    dve.wait_ge(spec_ps, k % 2 + 1)
                    tt(spec[:, k, :].rearrange("p (b d) -> p b d", b=G), bk[:, :].rearrange("p (b d) -> p b d", b=G),
                       kf[:, c_:c_ + 1, :].broadcast_to([P, G, D]), ALU.mult).then_inc(spec_mul, 1)

            def conv_d(m, g):
                dve.wait_ge(y_ps, 1)
                tt(xm, XC[:, :].rearrange("p (b d) -> p b d", b=G), film[:, :, 2 * D:3 * D], ALU.mult).then_inc(y_mod, 1)

            def ln2(m, g):
                dve.wait_ge(xt_ready, 1)
                stats(xt)

            def ln2_out(m, g):
                dve.wait_ge(ln_scales, 2)
                normalise(hh, xt, 5).then_inc(hh_ready, 1)

            def xmlp_b(m, g):
                dve.wait_ge(xo_ps, 1)
                tt(xt[:, :, :], XC[:, :].rearrange("p (b d) -> p b d", b=G), xt[:, :, :], ALU.add).then_inc(xo_add, 1)

            def ln3(m, g):
                dve.wait_ge(xt2_ready, 1)
                stats(xt)

            def ln3_out(m, g):
                dve.wait_ge(ln_scales, 3)
                normalise(hh, xt, 9).then_inc(n_ready, 1)

            def ln4(m, g):
                dve.wait_ge(xnew_ready, 1)
                stats(xnew)

            def ln4_out(m, g):
                dve.wait_ge(ln_scales, 4)
                normalise(hh, xnew, 13).then_inc(xf_ready, 1)
                normalise(xh, xnew, 15).then_inc(xf_ready, 1)

            def make(g, m):
                for c_ in range(n["made"], n["made"] + STEP):
                    dve.wait_ge(tanh_done, c_ + 1)
                    tt(ring[:, c_ % RING, :], ring[:, c_ % RING, :], ring[:, c_ % RING, :], ALU.mult).then_inc(basis_ready, 1)
                n["made"] += STEP

            def gate_a(g, m):
                dve.wait_ge(gl_ps, 1)
                dve.tensor_copy(gl[:, :, :].rearrange("p b e -> p (b e)"), V[:, 0:G * NX]).then_inc(gl_sb, 1)
                dve.wait_ge(gl_sb, 1)
                for b in range(G):
                    t = dve.max(gtop[:, b, :], gl[:, b, :])
                link(t)
                for b in range(G):
                    dve.max_index(gidx[:, b, :], gtop[:, b, :], gl[:, b, :])
                tt(gs[:, 0, :], gtop[:, :, 1], gtop[:, :, 0], ALU.subtract).then_inc(gdiff, 1)

            def gate_c(g, m):
                dve.wait_ge(gexp, 1)
                e2, den, w1, w2 = (gs[:, k, :] for k in (1, 2, 3, 4))
                link(dve.tensor_copy(gidf[:, :, :], gidx[:, :, :]))
                link(ts(den, e2, 1.0, None, ALU.add))
                link(dve.reciprocal(w1, den))
                link(ts(w1, w1, gtanh[:, 1:2], None, ALU.mult))
                link(tt(w2, e2, w1, ALU.mult))
                iota = misc[:, 1:9].unsqueeze(1).broadcast_to([P, G, NX])
                for k, w in ((0, w1), (1, w2)):
                    link(tt(gw[:, k], iota, gidf[:, :, k:k + 1].broadcast_to([P, G, NX]), ALU.is_equal))
                    link(tt(gw[:, k], gw[:, k], w.unsqueeze(2).broadcast_to([P, G, NX]), ALU.mult))
                link(tt(gw[:, 2], gw[:, 0], gw[:, 1], ALU.add))
                link(dve.tensor_copy(wp[:, :, 0, :], gw[:, 2]))
                link(tt(gw[:, 3], gw[:, 2], wp[:, :, 0, :], ALU.subtract))
                link(dve.tensor_copy(wp[:, :, 1, :], gw[:, 3]))
                link(tt(gw[:, 4], gw[:, 3], wp[:, :, 1, :], ALU.subtract))
                dve.tensor_copy(wp[:, :, 2, :], gw[:, 4]).then_inc(wp_ready, 1)

            def gate_d(g, m):
                dve.wait_ge(wt_ps, 1)
                dve.tensor_copy(wt[:, :], HA[0:3 * NX, 0:GT // 2].bitcast(BF16)).then_inc(wt_sb, 1)

            def z_out(g, m, e):
                dve.wait_ge(basis_used, Z_DONE[e])
                if e > 0:
                    dve.wait_ge(h1_ready, 2 * e)
                for h in range(2):
                    ts(zc[:, h, :], Z[h][:, :], -1.0, const0[:, e, h:h + 1], ALU.mult, ALU.add).then_inc(zc_ready, 1)

            def var_a(g, m, e):
                dve.wait_ge(var_ps, e + 1)
                ts(vv[:, 0, :], V[:, 0:G], EPS, None, ALU.add).then_inc(var_sb, 1)

            def var_b(g, m, e):
                dve.wait_ge(rstd_ready, e + 1)
                tt(dg[:, :, :], ident[:, :].unsqueeze(1).broadcast_to([P, G, P]),
                   vv[:, 1, :].unsqueeze(2).broadcast_to([P, G, P]), ALU.mult).then_inc(dg_ready, 1)

            def var_c(g, m, e):
                dve.wait_ge(rb_ps, e + 1)
                for h in range(2):
                    tt(h1[:, e % 2, h, :], zc[:, h, :], V[:, :], ALU.mult).then_inc(h1_ready, 1)

            def comb(g, m, i):
                x = OUTS[i]
                dve.wait_ge(*out_done(i))
                dve.wait_ge(wb_sb, i + 1)
                if i >= 2:
                    dve.wait_ge(acc_ready, i - 1)
                r = ROW_OF["L0_ffn_mlp_b2"] + x
                col, op = (cols[:, r:r + 1], ALU.add) if x < NE else (const1[:, x - NE:x - NE + 1], ALU.subtract)
                dve.scalar_tensor_tensor(out=part[:, i % 2, :], in0=O[:, :], scalar=col, in1=wbs[:, i % 3, :], op0=op,
                                         op1=ALU.mult).then_inc(part_ready, 1)

            def finish(g, m):
                dve.wait_ge(yt_ps, 1)
                dve.wait_ge(res_ready, 1)
                tt(yout, O[:, :].rearrange("p (b d) -> p b d", b=G), xres[:, :, :], ALU.add).then_inc(y_ready, 1)

            Z_DONE = [CHUNKS.index((e, 0, NG - 1)) + 1 for e in range(NE)]

            def out_done(i):
                x = OUTS[i]
                if x < NE:
                    return mg_used, HC * (x + 1)
                return basis_used, CHUNKS.index((x - NE, 1, 2 * NG - 1)) + 1

            steps = dict(s4_dt=s4_dt, s4_half=s4_half, s4_turn=s4_turn, s4_args=s4_args, s4_pow=s4_pow, kan0=kan0,
                         kan1=kan1, kan_const=kan_const, ln1=ln1, ln1_out=ln1_out, qk=qk, scores=scores, topk=topk, probs_a=probs_a, probs_c=probs_c,
                         attn_sum=attn_sum, modulate=modulate, conv_b=conv_b, conv_d=conv_d, ln2=ln2, ln2_out=ln2_out,
                         xmlp_b=xmlp_b, ln3=ln3, ln3_out=ln3_out, ln4=ln4, ln4_out=ln4_out, make=make, gate_a=gate_a,
                         gate_c=gate_c, gate_d=gate_d, z_out=z_out, var_a=var_a, var_b=var_b, var_c=var_c, comb=comb,
                         finish=finish)
            rounds(dve, "vector", steps, n)


def shape_constants():
    f, t = np.arange(P)[None, :], np.arange(S)[:, None]
    ang = np.pi * (2 * f + 1) * t / (2.0 * S)
    ang_i = ang.T
    dft = np.stack([np.cos(ang), -np.sin(ang), np.cos(ang_i) / S, -np.sin(ang_i) / S], axis=1)
    esel = np.zeros((3, NX, NX, P))
    for e in range(NX):
        esel[:, e, e, :] = 1.0
    misc = np.zeros((P, 17))
    misc[0:NST, 0] = 0.25
    misc[:, 1:9] = np.arange(NX)
    misc[:, 9:17] = -0.5 * np.linspace(-1.2, 0.2, NG).astype(np.float32)
    return {"c_dft": dft.astype(np.float32), "c_ident": np.eye(P, dtype=np.float32),
            "c_esel": esel.reshape(3 * NX, NX, P).astype(np.float32), "c_misc": misc.astype(np.float32)}


def kernel(**inputs):
    import concourse.bacc as _bacc
    from concourse.bass_utils import run_bass_kernel_spmd as _run

    nc = _bacc.Bacc("TRN2", target_bir_lowering=False, num_devices=1)
    names = {"mask_BxS_bf1": "mask_text", "mask_BxS2_bf1": "mask_vision"}
    arrays, aps = {}, {}
    for name, value in list(inputs.items()) + list(shape_constants().items()):
        v = np.ascontiguousarray(value)
        if v.dtype == np.bool_:
            v = v.view(np.uint8)
        if v.ndim == 0:
            v = v.reshape(1)
        name = names.get(name, name)
        arrays[f"in_{name}"] = v
        aps[name] = nc.dram_tensor(f"in_{name}", v.shape, mybir.dt.from_np(v.dtype), kind="ExternalInput").ap()
    out = nc.dram_tensor("out_0", tuple(inputs["x"].shape), F32, kind="ExternalOutput").ap()
    build(nc, aps, out)
    r = _run(nc, [arrays], core_ids=[0])
    return r.results[0]["out_0"]
```
